# Optimizing a Trainium2 kernel written in Bass

```python
import numpy as np
import jax
import jax.numpy as jnp

def _softmax(x, axis=-1):
    return jax.nn.softmax(x, axis=axis)

def _gelu(x):
    return jax.nn.gelu(x, approximate=True)

def _silu(x):
    return jax.nn.silu(x)

def _sigmoid(x):
    return jax.nn.sigmoid(x)

def _layernorm(x, axis=-1, eps=1e-05):
    m = jnp.mean(x, axis=axis, keepdims=True)
    v = jnp.var(x, axis=axis, keepdims=True)
    return (x - m) / jnp.sqrt(v + eps)

def _scatter_add(tgt, idx, src, axis=0):
    return tgt.at[idx].add(src)

def _segment_sum(src, seg, n):
    return jax.ops.segment_sum(src, seg, n)
kernel_name = 'mk_recurrent_d1_jaxref_r4_ebb39e'

def setup_inputs(seed: int=0):
    np.random.seed(seed)
    _w = jnp.asarray

    def _L0_attn_setup():
        import jax, jax.numpy as jnp
        import numpy as np
        H = 1024
        D_IN = 2048
        N = 16
        K = 4
        R = 64
        EPS = 1e-06

        def rms_forward(x, eps=EPS):
            xf = x.astype(jnp.float32)
            var = jnp.mean(xf * xf, axis=-1, keepdims=True)
            return (xf * jax.lax.rsqrt(var + eps)).astype(x.dtype)
        key = jax.random.key(seed)
        ks = jax.random.split(key, 10)
        s = 0.02
        hidden_states = jax.random.normal(ks[0], (2, 256, H), dtype=jnp.float32)
        W_in = jax.random.normal(ks[1], (2 * D_IN, H), dtype=jnp.float32) * s
        conv_w = jax.random.normal(ks[2], (D_IN, K), dtype=jnp.float32) * 0.2
        conv_b = jax.random.normal(ks[3], (D_IN,), dtype=jnp.float32) * 0.02
        W_x = jax.random.normal(ks[4], (R + 2 * N, D_IN), dtype=jnp.float32) * s
        W_dt = jax.random.normal(ks[5], (D_IN, R), dtype=jnp.float32) * s
        b_dt = jax.random.normal(ks[6], (D_IN,), dtype=jnp.float32) * 0.02
        A_log = jnp.log(jnp.broadcast_to(jnp.arange(1, N + 1, dtype=jnp.float32)[None, :], (D_IN, N)))
        D = jnp.ones((D_IN,), dtype=jnp.float32)
        W_out = jax.random.normal(ks[7], (H, D_IN), dtype=jnp.float32) * s
        return {'hidden_states': hidden_states, 'W_in': W_in, 'conv_w': conv_w, 'conv_b': conv_b, 'W_x': W_x, 'W_dt': W_dt, 'b_dt': b_dt, 'A_log': A_log, 'D': D, 'W_out': W_out}
    _L0_attn_in = _L0_attn_setup()

    def _L0_ffn_setup():
        import jax, jax.numpy as jnp
        import numpy as np
        B, S, D, F = (4, 512, 1024, 4096)
        key = jax.random.key(seed)
        k = jax.random.split(key, 5)
        scale_in = 1.0 / np.sqrt(D)
        scale_out = 1.0 / np.sqrt(F)
        return {'input': jax.random.normal(k[0], (B, S, D), dtype=jnp.float32), 'inter_w': jax.random.normal(k[1], (D, F), dtype=jnp.float32) * scale_in, 'inter_b': jax.random.normal(k[2], (F,), dtype=jnp.float32) * 0.02, 'output_w': jax.random.normal(k[3], (F, D), dtype=jnp.float32) * scale_out, 'output_b': jax.random.normal(k[4], (D,), dtype=jnp.float32) * 0.02}
    _L0_ffn_in = _L0_ffn_setup()
    _d = {'L0_attn_hidden_states': _L0_attn_in['hidden_states'], 'L0_attn_W_in': _L0_attn_in['W_in'], 'L0_attn_conv_w': _L0_attn_in['conv_w'], 'L0_attn_conv_b': _L0_attn_in['conv_b'], 'L0_attn_W_x': _L0_attn_in['W_x'], 'L0_attn_W_dt': _L0_attn_in['W_dt'], 'L0_attn_b_dt': _L0_attn_in['b_dt'], 'L0_attn_A_log': _L0_attn_in['A_log'], 'L0_attn_D': _L0_attn_in['D'], 'L0_attn_W_out': _L0_attn_in['W_out'], 'L0_ffn_inter_w': _L0_ffn_in['inter_w'], 'L0_ffn_inter_b': _L0_ffn_in['inter_b'], 'L0_ffn_output_w': _L0_ffn_in['output_w'], 'L0_ffn_output_b': _L0_ffn_in['output_b']}
    _x0 = _d['L0_attn_hidden_states']
    _d['L0_attn_hidden_states'] = jax.random.normal(jax.random.fold_in(jax.random.key(seed), 1), (2, 1024, 1024), dtype=_x0.dtype)
    del _x0
    return _d

def reference(L0_attn_hidden_states, L0_attn_W_in, L0_attn_conv_w, L0_attn_conv_b, L0_attn_W_x, L0_attn_W_dt, L0_attn_b_dt, L0_attn_A_log, L0_attn_D, L0_attn_W_out, L0_ffn_inter_w, L0_ffn_inter_b, L0_ffn_output_w, L0_ffn_output_b):

    def _L0_attn_ref(hidden_states, W_in, conv_w, conv_b, W_x, W_dt, b_dt, A_log, D, W_out):
        import jax, jax.numpy as jnp
        import numpy as np
        H = 1024
        D_IN = 2048
        N = 16
        K = 4
        R = 64
        EPS = 1e-06

        def rms_forward(x, eps=EPS):
            xf = x.astype(jnp.float32)
            var = jnp.mean(xf * xf, axis=-1, keepdims=True)
            return (xf * jax.lax.rsqrt(var + eps)).astype(x.dtype)
        b, L, _ = hidden_states.shape
        proj = hidden_states @ W_in.T
        x, gate = (proj[..., :D_IN], proj[..., D_IN:])
        xpad = jnp.pad(x, ((0, 0), (K - 1, 0), (0, 0)))
        xc = conv_b
        for j in range(K):
            xc = xc + conv_w[:, j] * xpad[:, j:j + L, :]
        x = jax.nn.silu(xc)
        ssm = x @ W_x.T
        ts, Bm, Cm = (ssm[..., :R], ssm[..., R:R + N], ssm[..., R + N:])
        ts = rms_forward(ts)
        Bm = rms_forward(Bm)
        Cm = rms_forward(Cm)
        dt = jax.nn.softplus(ts @ W_dt.T + b_dt)
        A = -jnp.exp(A_log.astype(jnp.float32))

        def step(state, inp):
            dt_t, B_t, C_t, u_t = inp
            dA = jnp.exp(dt_t[..., None] * A)
            state = state * dA + (dt_t * u_t)[..., None] * B_t[:, None, :]
            y = jnp.einsum('bdn,bn->bd', state, C_t)
            return (state, y)
        init = jnp.zeros((b, D_IN, N), dtype=jnp.float32)
        xs = (dt.transpose(1, 0, 2), Bm.transpose(1, 0, 2), Cm.transpose(1, 0, 2), x.transpose(1, 0, 2))
        _, ys = jax.lax.scan(step, init, xs)
        y = ys.transpose(1, 0, 2) + x * D
        y = y * jax.nn.silu(gate)
        return y @ W_out.T

    def _L0_ffn_ref(input, inter_w, inter_b, output_w, output_b):
        import jax, jax.numpy as jnp
        import numpy as np
        B, S, D, F = (4, 512, 1024, 4096)
        h = jax.nn.gelu(jnp.einsum('bsd,df->bsf', input, inter_w) + inter_b, approximate=True)
        out = jnp.einsum('bsf,fd->bsd', h, output_w) + output_b
        return out
    x = L0_attn_hidden_states
    xn = _layernorm(x, axis=-1)
    s = _L0_attn_ref(xn, L0_attn_W_in, L0_attn_conv_w, L0_attn_conv_b, L0_attn_W_x, L0_attn_W_dt, L0_attn_b_dt, L0_attn_A_log, L0_attn_D, L0_attn_W_out)
    g = _silu(_L0_ffn_ref(xn, L0_ffn_inter_w, L0_ffn_inter_b, L0_ffn_output_w, L0_ffn_output_b))
    x = x + s * g
    return x

_drawn_inputs = setup_inputs


def setup_inputs(seed=0):
    import zlib

    import numpy as np

    out = dict(_drawn_inputs(seed))
    spreads = {'L0_attn_D': (1.0, 0.6)}
    factors = {'L0_attn_conv_b': 8.0,
     'L0_attn_W_dt': 8.0,
     'L0_attn_b_dt': 53.102,
     'L0_attn_A_log': 20.406,
     'L0_ffn_inter_b': 25.248,
     'L0_ffn_output_b': 8.0}
    for name, (base, spread) in spreads.items():
        noise = np.random.default_rng([zlib.crc32(name.encode()), seed]).standard_normal(out[name].shape)
        drawn = base * np.exp(spread * noise) if base else spread * noise
        out[name] = jnp.asarray(drawn.astype(out[name].dtype))
    for name, factor in factors.items():
        out[name] = (out[name] * factor).astype(out[name].dtype)
    return out
```

```python
from contextlib import ExitStack

import concourse.bass as bass
from concourse import mybir

F32 = mybir.dt.float32
ALU = mybir.AluOpType
ACT = mybir.ActivationFunctionType
AX = mybir.AxisListType

P = 128
H = 1024
D_IN = 2048
N = 16
K = 4
R = 64
F = 4096
B, L = 2, 1024
T = B * L
LN_EPS, RMS_EPS = 1e-5, 1e-6

TC = 512
NCH = T // TC
CPB = L // TC
HT = H // P
DT = D_IN // P
FT = F // P
GRP = 8
STEPS = 16
S4 = 4
TS = 256
Q = 4
NQ = N // Q
SROWS = R + 2 * N
NW = 4
NM = 4

C_CONVW = 0
C_CONVB = C_CONVW + DT * K
C_BDT = C_CONVB + DT
C_D = C_BDT + DT
C_ALOG = C_D + DT
C_B1 = C_ALOG + DT * N
C_B2 = C_B1 + FT
C_ONES = C_B2 + HT
C_BLK = C_ONES + P
C_EPS = C_BLK + SROWS
NPAR = C_EPS + 2


def w_per_step(c):
    return 4 + (2 if c < NCH - 1 else 0) + (1 if c > 0 else 0)


def m_per_step(c):
    return 4 + (2 if c < NCH - 1 else 0)


PRE_TILES = 2 * DT
W_BASE = [PRE_TILES + STEPS * sum(w_per_step(b) for b in range(c)) for c in range(NCH + 1)]
M_BASE = [PRE_TILES + STEPS * sum(m_per_step(b) for b in range(c)) for c in range(NCH + 1)]
assert all(b % NW == 0 for b in W_BASE) and all(b % NM == 0 for b in M_BASE)


class Ring:

    def __init__(self, base, per, n):
        self.base, self.per, self.n = base, per, n

    def slot(self, off):
        return off % self.n

    def turn(self, g, off):
        return g * (self.per * S4 // self.n) + (self.base // self.n + off // self.n)

    def number(self, g, off):
        return g * (self.per * S4) + (self.base + off)


def build(nc, xT, params, w_x, w_g, w_1, w_2, w_o, w_ssm, w_dt, outT):
    spill = nc.dram_tensor("spill", (DT, P, 3, T), F32, kind="Internal").ap()
    y_d = nc.dram_tensor("y_d", (DT, P, T), F32, kind="Internal").ap()
    g_d = nc.dram_tensor("g_d", (HT, P, T), F32, kind="Internal").ap()
    bc_d = nc.dram_tensor("bc_d", (2 * N, T), F32, kind="Internal").ap()

    ctx = ExitStack()
    with ctx:
        def sb(name, shape):
            return ctx.enter_context(nc.sbuf_tensor(name, shape, F32))

        def ps(name):
            return ctx.enter_context(nc.psum_tensor(name, [P, TC], F32))

        def sem(name):
            return ctx.enter_context(nc.semaphore(name))

        def sems(name, n):
            return [sem(f"{name}{i}") for i in range(n)]

        par = sb("par", [P, NPAR])
        xn = [sb(f"xn{i}", [P, HT, TC]) for i in range(2)]
        wts = sb("wts", [P, NW, 8, P])
        hid = sb("hid", [P, GRP, TC])
        facc = sb("facc", [P, HT, TC])
        yin = sb("yin", [P, DT, TC])
        bbc = sb("bbc", [P, N, TS])
        cbc = sb("cbc", [P, N, TS])
        work = sb("work", [P, N, TS + 1])
        decay = sb("decay", [P, 2, Q, TS + 1])
        unit = sb("unit", [P, 2, 3, TS])
        dtu = sb("dtu", [P, TS])
        yt = sb("yt", [P, 2, TS])
        xin = sb("xin", [P, 2, K - 1 + TC])
        ut = sb("ut", [P, 2, TC])
        dtb = sb("dtb", [P, 5, TC])
        ssm = sb("ssm", [SROWS, TC])
        gx = sb("gx", [P, 2, TC])
        wssm = sb("wssm", [P, 2, SROWS])
        wdt = sb("wdt", [R, 2, P])
        aneg = sb("aneg", [P, DT * N])
        carry = sb("carry", [P, DT, N])
        halo = sb("halo", [P, DT, K - 1])
        zeros = sb("zeros", [P, K])

        pm = [ps(f"pm{i}") for i in range(NM)]
        p_out, p_ssm = ps("p_out"), ps("p_ssm")
        p_st = [ps("p_st0"), ps("p_st1")]

        params_in, zeros_set, aneg_exp, aneg_full = sem("params_in"), sem("zeros_set"), sem("aneg_exp"), sem("aneg_full")
        w_full, product_done, evacuated = sems("w_full", NW), sem("product_done"), sems("evacuated", NM)
        x_in, mean_full, centered = sems("x_in", 2), sem("mean_full"), sem("centered")
        sq_full, sq_used, var_full, std_full = sem("sq_full"), sem("sq_used"), sem("var_full"), sem("std_full")
        rstd_full, xn_ready = sem("rstd_full"), sem("xn_ready")
        conv_tap, conv_done = sem("conv_tap"), sem("conv_done")
        u_full, gate_full, ut_stored = sem("u_full"), sem("gate_full"), sems("ut_stored", 2)
        wssm_full, wssm_used, wdt_full = sems("wssm_full", 2), sem("wssm_used"), sems("wdt_full", 2)
        ssm_full, ssm_evac, ssq_full, ms_full = sem("ssm_full"), sem("ssm_evac"), sem("ssq_full"), sem("ms_full")
        srs_full, srs_inv, ssm_ready, bc_stored = sem("srs_full"), sem("srs_inv"), sem("ssm_ready"), sem("bc_stored")
        dt_full, dt_bank_free, dt_chain = sem("dt_full"), sem("dt_bank_free"), sem("dt_chain")
        dt_pool, dt_stored = sem("dt_pool"), sem("dt_stored")
        b_full, c_full, unit_in = sem("b_full"), sem("c_full"), sems("unit_in", 2)
        decay_full, decay_free = sem("decay_full"), sem("decay_free")
        dtu_full, driven, carried, weighted = sem("dtu_full"), sem("driven"), sem("carried"), sem("weighted")
        summed, skipped, unit_done, y_stored = sem("summed"), sem("skipped"), sem("unit_done"), sems("y_stored", 2)
        h_full, facc_zero, g_full, g_stored = sem("h_full"), sem("facc_zero"), sem("g_full"), sem("g_stored")
        y_in, d_full, d_free = sem("y_in"), sem("d_full"), sem("d_free")
        gx_in, out_ready, out_stored = sem("gx_in"), sem("out_ready"), sem("out_stored")

        waits_met = sem("waits_met")

        DONE = 3
        W_DONE = NW + 1

        def col(base, i=0, n=1):
            return par[:, base + i:base + i + n]

        def toks(e):
            return slice(e * TC, (e + 1) * TC)

        def chan(g, s, k):
            return g * (2 * S4) + (2 * s + k)

        def unit_no(c, half, g, s, k):
            return g * (2 * S4) + (c * 2 * STEPS + half * STEPS + 2 * s + k)

        def turn2(e, g, s, per=8, base=0):
            return g * S4 + (e * per + base + s)

        def m_off(c, s, k, ffn):
            return s * m_per_step(c) + (m_per_step(c) - 4 if ffn else 0) + k

        def w_off(c, s, kind, k=0):
            inputs = 2 if c < NCH - 1 else 0
            return s * w_per_step(c) + {"in": 0, "ffn": inputs, "out": inputs + 4}[kind] + k

        def w_ring(c, half):
            return Ring(W_BASE[c] + half * 8 * w_per_step(c), w_per_step(c), NW)

        def m_ring(c, half):
            return Ring(M_BASE[c] + half * 8 * m_per_step(c), m_per_step(c), NM)

        def pre_ring(half):
            return Ring(half * DT, 2, NW)

        last_ring = Ring(W_BASE[NCH], 1, NW)

        def wait(eng, semaphore, count):
            eng.wait_ge(semaphore, count)
            if not isinstance(count, int):
                eng.sem_inc(waits_met, 1)

        block = ctx.enter_context(nc.Block())

        @block.sync
        def _(sp):
            def weight(ring, g, off, src):
                slot = ring.slot(off)
                wait(sp, product_done, ring.number(g, off) + 1)
                sp.dma_start(wts[:, slot].rearrange("p k m -> p (k m)"), src).then_inc(w_full[slot], 16)

            def ssm_weights(e, g, s):
                for k in range(2):
                    wait(sp, wssm_used, chan(g, s, k) + (e * DT + 1))
                    sp.dma_start(wssm[:, k], w_ssm[chan(g, s, k)]).then_inc(wssm_full[k], 16)

            def dt_weights(e, g, s):
                for k in range(2):
                    wait(sp, dt_bank_free, chan(g, s, k) + (e * DT + 1))
                    sp.dma_start(wdt[:, k], w_dt[chan(g, s, k)]).then_inc(wdt_full[k], 16)

            def x_chunk(e):
                sp.dma_start(xn[e % 2][:, :, :], xT[:, :, toks(e)].rearrange("k p t -> p k t")).then_inc(x_in[e % 2], 16)

            def scan_unit(c, half, g, s, k):
                wait(sp, unit_done, unit_no(c, half, g, s, k) + 1)
                if half == 0:
                    wait(sp, ut_stored[k], 16 * (turn2(c, g, s, 16, 8) + 2))
                    wait(sp, dt_stored, 16 * (chan(g, s, k) + (c * DT + 2)))
                t0 = c * TC + half * TS
                sp.dma_start(unit[:, k], spill[chan(g, s, k), :, :, t0:t0 + TS]).then_inc(unit_in[k], 16)

            sp.dma_start(par[:, :], params).then_inc(params_in, 16)
            x_chunk(0)
            x_chunk(1)
            for half in range(2):
                ring = pre_ring(half)
                with sp.Fori(0, 2) as g:
                    for s in range(S4):
                        for k in range(2):
                            weight(ring, g, 2 * s + k, (w_x if half == 0 else w_g)[chan(g, s, k)])
                        (ssm_weights if half == 0 else dt_weights)(0, g, s)

            for c in range(NCH):
                for half in range(2):
                    ring = w_ring(c, half)
                    with sp.Fori(0, 2) as g:
                        for s in range(S4):
                            if c < NCH - 1:
                                (ssm_weights if half == 0 else dt_weights)(c + 1, g, s)
                                for k in range(2):
                                    weight(ring, g, w_off(c, s, "in", k), (w_x if half == 0 else w_g)[chan(g, s, k)])
                            scan_unit(c, half, g, s, 0)
                            for k in range(4):
                                f = g * GRP + (2 * half * GRP + 4 * (s % 2) + k)
                                weight(ring, g, w_off(c, s, "ffn", k), (w_1 if s < 2 else w_2)[f])
                            scan_unit(c, half, g, s, 1)
                            if c > 0:
                                weight(ring, g, w_off(c, s, "out"), w_o[g * S4 + (2 * half * S4 + s)])
                if c + 2 < NCH:
                    wait(sp, product_done, w_ring(c, 1).number(1, w_off(c, 1, "ffn", 3)) + W_DONE)
                    x_chunk(c + 2)
            with sp.Fori(0, 4) as g:
                for s in range(S4):
                    weight(last_ring, g, s, w_o[g * S4 + s])

        @block.tensor
        def _(pe):
            def product(out, ring, g, off, rhs, start=True, stop=True):
                slot = ring.slot(off)
                pe.wait_ge(w_full[slot], 16 * (ring.turn(g, off) + 1))
                for k in range(8):
                    mm = pe.matmul(out, lhsT=wts[:, slot, k], rhs=rhs[:, k],
                                   start=start and k == 0, stop=stop and k == 7)
                mm.then_inc(product_done, 1)

            def ring_product(wring, mring, g, woff, moff, rhs):
                b = mring.slot(moff)
                pe.wait_ge(evacuated[b], mring.turn(g, moff) + 1)
                product(pm[b][:, :], wring, g, woff, rhs)

            def out_product(wring, g, woff, e, s, base=0):
                if s % 2 == 0:
                    pe.wait_ge(y_in, 16 * (e + 1))
                    pe.wait_ge(d_free, g * 2 + (HT * e + base + s // 2 + 1))
                product(p_out[:, :], wring, g, woff, yin[:, 8 * (s % 2):8 * (s % 2) + 8],
                        start=s % 2 == 0, stop=s % 2 == 1)

            def layernorm_sums(e):
                pe.wait_ge(x_in[e % 2], 16 * (e // 2 + 1))
                for k in range(HT):
                    mm = pe.matmul(p_st[0][:, :], lhsT=col(C_ONES, 0, P), rhs=xn[e % 2][:, k],
                                   start=k == 0, stop=k == HT - 1)
                mm.then_inc(mean_full, 1)
                for k in range(HT):
                    pe.wait_ge(sq_full, HT * e + k + 1)
                    pe.matmul(p_st[1][:, :], lhsT=col(C_ONES, 0, P), rhs=dtb[:, k % 2],
                              start=k == 0, stop=k == HT - 1).then_inc(sq_used, 1)

            def ssm_open(e):
                if e == 0:
                    pe.wait_ge(zeros_set, 1)
                if e > 0:
                    pe.wait_ge(srs_full, e)
                pe.matmul(p_ssm[0:SROWS, :], lhsT=col(C_BLK, 0, SROWS), rhs=zeros[:, 0:1].to_broadcast([P, TC]), start=True, stop=False,
                          skip_group_check=True)

            def ssm_close(e):
                pe.matmul(p_ssm[0:SROWS, :], lhsT=col(C_BLK, 0, SROWS), rhs=zeros[:, 0:1].to_broadcast([P, TC]), start=False, stop=True,
                          skip_group_check=True).then_inc(ssm_full, 1)

            def ssm_products(e, g, s):
                for k in range(2):
                    pe.wait_ge(wssm_full[k], 16 * (turn2(e, g, s) + 1))
                    pe.wait_ge(u_full, chan(g, s, k) + (e * DT + 1))
                    pe.matmul(p_ssm[0:SROWS, :], lhsT=wssm[:, k], rhs=ut[:, k], start=False, stop=False,
                              skip_group_check=True).then_inc(wssm_used, 1)

            def ssm_square_means(e):
                pe.wait_ge(ssq_full, e + 1)
                pe.matmul(p_ssm[0:SROWS, :], lhsT=par[0:SROWS, C_BLK:C_BLK + SROWS],
                          rhs=dtb[0:SROWS, 0], start=True, stop=True).then_inc(ms_full, 1)

            def dt_product(e, g, s, k):
                n = chan(g, s, k) + e * DT
                pe.wait_ge(wdt_full[k], 16 * (turn2(e, g, s) + 1))
                pe.wait_ge(ssm_ready, e + 1)
                pe.wait_ge(dt_bank_free, n + 1)
                pe.matmul(p_st[k][:, :], lhsT=wdt[:, k], rhs=ssm[0:R, :], start=True, stop=True)\
                    .then_inc(dt_full, 1)

            pe.wait_ge(params_in, 16)
            layernorm_sums(0)
            pe.wait_ge(xn_ready, 1)
            ssm_open(0)
            ring = pre_ring(0)
            with pe.Fori(0, 2) as g:
                for s in range(S4):
                    for k in range(2):
                        ring_product(ring, ring, g, 2 * s + k, 2 * s + k, xn[0])
                    if s > 0:
                        ssm_products(0, g, s - 1)
                ssm_products(0, g, S4 - 1)
            layernorm_sums(1)
            ssm_close(0)
            ssm_square_means(0)
            ring = pre_ring(1)
            with pe.Fori(0, 2) as g:
                for s in range(S4):
                    for k in range(2):
                        ring_product(ring, ring, g, 2 * s + k, 2 * s + k, xn[0])
                    dt_product(0, g, s, 0)
                    dt_product(0, g, s, 1)

            for c in range(NCH):
                pe.wait_ge(xn_ready, min(c + 2, NCH))
                if c < NCH - 1:
                    ssm_open(c + 1)
                for half in range(2):
                    wring, mring = w_ring(c, half), m_ring(c, half)
                    with pe.Fori(0, 2) as g:
                        for s in range(S4):
                            if c < NCH - 1:
                                for k in range(2):
                                    ring_product(wring, mring, g, w_off(c, s, "in", k), m_off(c, s, k, False),
                                                 xn[(c + 1) % 2])
                            for k in range(4):
                                if s == 2 and k == 0:
                                    pe.wait_ge(h_full, g * 2 + (c * 8 + half * 4 + 2))
                                ring_product(wring, mring, g, w_off(c, s, "ffn", k), m_off(c, s, k, True),
                                             xn[c % 2] if s < 2 else hid)
                                if c < NCH - 1 and half == 1 and k % 2:
                                    dt_product(c + 1, g, s, k // 2)
                            if c < NCH - 1 and half == 0:
                                ssm_products(c + 1, g, s)
                            if c > 0:
                                out_product(wring, g, w_off(c, s, "out"), c - 1, s, 4 * half)
                    if c < NCH - 1 and half == 0:
                        ssm_close(c + 1)
                        ssm_square_means(c + 1)
                if c + 2 < NCH:
                    pe.wait_ge(dt_bank_free, 2 + DT * (c + 2))
                    layernorm_sums(c + 2)
            with pe.Fori(0, 4) as g:
                for s in range(S4):
                    out_product(last_ring, g, s, NCH - 1, s)

        @block.scalar
        def _(act):
            def decays(c, half, g, s, k, quarters):
                U = unit_no(c, half, g, s, k)
                if quarters[0] == 0:
                    act.wait_ge(unit_in[k], 16 * (turn2(c, g, s, STEPS, 8 * half) + 1))
                for q in quarters:
                    act.wait_ge(decay_free, U * 4 + (q + 1))
                    for i in range(Q):
                        a = chan(g, s, k) * N + (q * Q + i)
                        ins = act.activation(decay[:, q % 2, i, 1:], unit[:, k, 0], ACT.Exp, scale=aneg[:, bass.ds(a, 1)])
                    ins.then_inc(decay_full, 1)

            def input_tile(e, half, g, s, k, wring, woff, mring, moff):
                b = mring.slot(moff)
                ch = chan(g, s, k)
                act.wait_ge(product_done, wring.number(g, woff) + W_DONE)
                if half == 0:
                    act.wait_ge(conv_done, ch + (e * DT + 1))
                    first = e % CPB == 0
                    act.activation(xin[:, k, 0:K - 1], zeros[:, 0:K - 1] if first else halo[:, ch], ACT.Copy)
                    if first:
                        act.activation(halo[:, ch], pm[b][:, TC - K + 1:TC], ACT.Copy)
                    act.activation(xin[:, k, K - 1:], pm[b][:, :], ACT.Copy).then_inc(evacuated[b], 1)
                else:
                    act.wait_ge(ut_stored[k], 16 * (turn2(e, g, s, 16, 8) + 1))
                    act.activation(ut[:, k], pm[b][:, :], ACT.Copy).then_inc(evacuated[b], 1)

            def input_silu(e, half, g, s, mring, moff):
                for k in range(2):
                    ch = chan(g, s, k)
                    if half == 0:
                        act.wait_ge(conv_done, ch + (e * DT + DONE))
                        act.activation(ut[:, k], ut[:, k], ACT.Silu, bias=par[:, bass.ds(ch + C_CONVB, 1)])\
                            .then_inc(u_full, 1)
                    else:
                        act.wait_ge(evacuated[mring.slot(moff + k)], mring.turn(g, moff + k) + 2)
                        act.activation(ut[:, k], ut[:, k], ACT.Silu).then_inc(gate_full, 1)

            def hidden_tile(c, half, g, s, k):
                wring, mring = w_ring(c, half), m_ring(c, half)
                b = mring.slot(m_off(c, s, k, True))
                act.wait_ge(product_done, wring.number(g, w_off(c, s, "ffn", k)) + W_DONE)
                act.activation(hid[:, 4 * s + k], pm[b][:, :], ACT.Identity,
                               bias=par[:, bass.ds(g * GRP + (C_B1 + 2 * half * GRP + 4 * s + k), 1)])\
                    .then_inc(evacuated[b], 1)

            def dt_tile(e, g, s, k):
                ch = chan(g, s, k)
                n = ch + e * DT
                bias = par[:, bass.ds(ch + C_BDT, 1)]
                act.wait_ge(dt_full, n + 1)
                act.wait_ge(dt_pool, n * 3 + 3)
                act.activation(dtb[:, 0], p_st[k][:, :], ACT.Relu, bias=bias)
                act.activation(dtb[:, 1], p_st[k][:, :], ACT.Abs, bias=bias).then_inc(dt_bank_free, 1)
                act.wait_ge(dt_bank_free, n + DONE)
                act.activation(dtb[:, 1], dtb[:, 1], ACT.Exp, scale=-1.0).then_inc(dt_chain, 1)
                act.wait_ge(dt_chain, n * 4 + 1)
                act.activation(dtb[:, 2], dtb[:, 1], ACT.Identity, bias=1.0).then_inc(dt_chain, 1)
                act.wait_ge(dt_chain, n * 4 + 2)
                act.activation(dtb[:, 3], dtb[:, 2], ACT.Ln).then_inc(dt_chain, 1)
                act.wait_ge(dt_chain, n * 4 + 3)
                act.activation(dtb[:, 2], dtb[:, 2], ACT.Identity, bias=-1.0).then_inc(dt_chain, 1)

            def ssm_norm(e):
                act.wait_ge(ssm_full, e + 1)
                if e > 0:
                    act.wait_ge(bc_stored, 16 * e)
                    act.wait_ge(xn_ready, e + 1)
                act.activation(ssm[:, :], p_ssm[0:SROWS, :], ACT.Copy).then_inc(ssm_evac, 1)
                act.wait_ge(ssm_evac, e + 1)
                act.activation(dtb[0:SROWS, 0], ssm[:, :], ACT.Square).then_inc(ssq_full, 1)
                act.wait_ge(ms_full, e + 1)
                act.activation(dtb[0:SROWS, 2], p_ssm[0:SROWS, :], ACT.Sqrt, bias=par[0:SROWS, C_EPS + 1:C_EPS + 2])\
                    .then_inc(srs_full, 1)
                act.wait_ge(ssm_ready, e + 1)

            def layernorm(e):
                if e >= 2:
                    act.wait_ge(dt_pool, 3 * (DT * e + 1))
                for k in range(HT):
                    if k >= 2:
                        act.wait_ge(sq_used, HT * e + k - 1)
                    act.wait_ge(centered, HT * e + k + 1)
                    act.activation(dtb[:, k % 2], xn[e % 2][:, k], ACT.Square).then_inc(sq_full, 1)
                act.wait_ge(sq_used, HT * (e + 1))
                act.activation(dtb[:, 2], p_st[1][:, :], ACT.Sqrt, bias=col(C_EPS)).then_inc(std_full, 1)

            act.wait_ge(params_in, 16)
            act.activation(aneg[:, :], col(C_ALOG, 0, DT * N), ACT.Exp).then_inc(aneg_exp, 1)
            layernorm(0)
            act.wait_ge(zeros_set, 1)
            for half in range(2):
                ring = pre_ring(half)
                with act.Fori(0, 2) as g:
                    for s in range(S4):
                        for k in range(2):
                            input_tile(0, half, g, s, k, ring, 2 * s + k, ring, 2 * s + k)
                        if half == 1:
                            dt_tile(0, g, s, 0)
                        input_silu(0, half, g, s, ring, 2 * s)
                        if half == 1:
                            dt_tile(0, g, s, 1)
                if half == 0:
                    layernorm(1)
                    act.wait_ge(xn_ready, 2)
                    ssm_norm(0)
            act.wait_ge(aneg_full, 1)

            for c in range(NCH):
                more = c < NCH - 1
                for half in range(2):
                    wring, mring = w_ring(c, half), m_ring(c, half)
                    with act.Fori(0, 2) as g:
                        for s in range(S4):
                            decays(c, half, g, s, 0, (0, 1))
                            if more:
                                for k in range(2):
                                    input_tile(c + 1, half, g, s, k, wring, w_off(c, s, "in", k), mring, m_off(c, s, k, False))
                            decays(c, half, g, s, 0, (2, 3))
                            if more:
                                input_silu(c + 1, half, g, s, mring, m_off(c, s, 0, False))
                            if s < 2:
                                hidden_tile(c, half, g, s, 0)
                                hidden_tile(c, half, g, s, 1)
                            if more and half == 1:
                                dt_tile(c + 1, g, s, 0)
                            decays(c, half, g, s, 1, (0, 1))
                            if s < 2:
                                hidden_tile(c, half, g, s, 2)
                                hidden_tile(c, half, g, s, 3)
                            decays(c, half, g, s, 1, (2, 3))
                            if more and half == 1:
                                dt_tile(c + 1, g, s, 1)
                            if s < 2:
                                moff = m_off(c, s, 3, True)
                                act.wait_ge(evacuated[mring.slot(moff)], mring.turn(g, moff) + 2)
                                act.activation(hid[:, 4 * s:4 * s + 4], hid[:, 4 * s:4 * s + 4], ACT.Gelu_apprx_tanh)\
                                    .then_inc(h_full, 1)
                    if more and half == 0:
                        ssm_norm(c + 1)
                if c + 2 < NCH:
                    layernorm(c + 2)
                act.wait_ge(evacuated[NM - 1], M_BASE[c + 1] // NM + 1)
                for m in range(HT):
                    ins = act.activation(facc[:, m], facc[:, m], ACT.Silu, bias=col(C_B2, m))
                ins.then_inc(g_full, 1)

        @block.vector
        def _(dve):
            def quarter_drives(c, half, U, q):
                dve.tensor_tensor(work[:, q * Q:(q + 1) * Q, 1:], bbc[:, q * Q:(q + 1) * Q, :],
                                  dtu[:, :].unsqueeze(1).to_broadcast([P, Q, TS]), ALU.mult).then_inc(driven, 1)

            def quarter_scan(U, q):
                dve.wait_ge(driven, U * 4 + (q + 1))
                dve.wait_ge(decay_full, U * 4 + (q + 1))
                flat = work[:, q * Q:(q + 1) * Q, :].rearrange("p n t -> p (n t)")
                dve.tensor_tensor_scan(flat, decay[:, q % 2].rearrange("p n t -> p (n t)"), flat, 0.0,
                                       ALU.mult, ALU.add).then_inc(decay_free, 1)

            def scan_first(c, half, g, s, k):
                U = unit_no(c, half, g, s, k)
                dve.wait_ge(unit_in[k], 16 * (turn2(c, g, s, STEPS, 8 * half) + 1))
                dve.tensor_tensor(dtu[:, :], unit[:, k, 0], unit[:, k, 1], ALU.mult).then_inc(dtu_full, 1)
                if c % CPB == 0 and half == 0:
                    dve.memset(work[:, :, 0:1], 0.0)
                else:
                    dve.tensor_scalar(work[:, :, 0:1], carry[:, chan(g, s, k)].unsqueeze(2), 1.0, None, ALU.mult)
                dve.wait_ge(b_full, 16 * (2 * c + half + 1))
                dve.wait_ge(dtu_full, U + 1)
                quarter_drives(c, half, U, 0)
                quarter_drives(c, half, U, 1)
                quarter_scan(U, 0)
                quarter_drives(c, half, U, 2)
                quarter_scan(U, 1)

            def scan_rest(c, half, g, s, k):
                U = unit_no(c, half, g, s, k)
                quarter_drives(c, half, U, 3)
                quarter_scan(U, 2)
                quarter_scan(U, 3)
                dve.wait_ge(decay_free, U * 4 + (4 + 2))
                dve.tensor_scalar(carry[:, chan(g, s, k)].unsqueeze(2), work[:, :, TS:], 1.0, None, ALU.mult)\
                    .then_inc(carried, 1)
                dve.wait_ge(carried, U + 1)
                dve.wait_ge(c_full, 16 * (2 * c + half + 1))
                dve.tensor_tensor(work[:, :, 1:], work[:, :, 1:], cbc[:, :, :], ALU.mult).then_inc(weighted, 1)
                dve.wait_ge(weighted, U + 1)
                dve.wait_ge(y_stored[k], 16 * (turn2(c, g, s, STEPS, 8 * half) + 1))
                dve.tensor_reduce(yt[:, k], work[:, :, 1:].rearrange("p n t -> p t n"), AX.X, ALU.add)\
                    .then_inc(summed, 1)
                dve.wait_ge(summed, U + 1)
                dve.scalar_tensor_tensor(out=yt[:, k], in0=unit[:, k, 1], scalar=par[:, bass.ds(chan(g, s, k) + C_D, 1)],
                                         in1=yt[:, k], op0=ALU.mult, op1=ALU.add).then_inc(skipped, 1)
                dve.wait_ge(skipped, U + 1)
                dve.tensor_tensor(yt[:, k], yt[:, k], unit[:, k, 2], ALU.mult).then_inc(unit_done, 1)

            def convolution(e, g, s, mring, moff):
                pair = g * S4 + (e * 8 + s)
                for j in range(K):
                    for k in range(2):
                        ch = chan(g, s, k)
                        w = par[:, bass.ds(ch * K + (C_CONVW + j), 1)]
                        if j == 0:
                            dve.wait_ge(evacuated[mring.slot(moff + k)], mring.turn(g, moff + k) + 2)
                            dve.wait_ge(ut_stored[k], 16 * (turn2(e, g, s, 16) + 1))
                            dve.wait_ge(wssm_used, ch + (e * DT + 1))
                            ins = dve.tensor_scalar(ut[:, k], xin[:, k, 0:TC], w, None, ALU.mult)
                        else:
                            dve.wait_ge(conv_tap, pair * 6 + (2 * (j - 1) + k + 1))
                            ins = dve.scalar_tensor_tensor(out=ut[:, k], in0=xin[:, k, j:j + TC], scalar=w,
                                                           in1=ut[:, k], op0=ALU.mult, op1=ALU.add)
                        ins.then_inc(conv_tap if j < K - 1 else conv_done, 1)

            def output_add(c, half, g, s, k):
                wring, mring = w_ring(c, half), m_ring(c, half)
                b = mring.slot(m_off(c, s, k, True))
                m = 4 * (s - 2) + k
                dve.wait_ge(product_done, wring.number(g, w_off(c, s, "ffn", k)) + W_DONE)
                dve.wait_ge(facc_zero, c + 1)
                dve.tensor_tensor(facc[:, m], pm[b][:, :], facc[:, m], ALU.add).then_inc(evacuated[b], 1)

            def combine(ring, off, e, g, s, base):
                idx = g * 2 + (HT * e + base + s // 2)
                dve.wait_ge(product_done, ring.number(g, off) + W_DONE)
                dve.wait_ge(gx_in, idx * 32 + 32)
                dve.tensor_tensor(gx[:, 0], p_out[:, :], gx[:, 0], ALU.mult).then_inc(d_free, 1)
                dve.wait_ge(d_free, idx + 2)
                dve.tensor_tensor(gx[:, 0], gx[:, 0], gx[:, 1], ALU.add).then_inc(out_ready, 1)

            def layernorm(e):
                x = xn[e % 2][:, :, :]
                dve.wait_ge(mean_full, e + 1)
                for k in range(HT):
                    dve.tensor_tensor(xn[e % 2][:, k], xn[e % 2][:, k], p_st[0][:, :], ALU.subtract).then_inc(centered, 1)
                dve.wait_ge(std_full, e + 1)
                dve.reciprocal(dtb[:, 2], dtb[:, 2]).then_inc(rstd_full, 1)
                dve.wait_ge(rstd_full, e + 1)
                dve.tensor_tensor(x, x, dtb[:, 2].unsqueeze(1).to_broadcast([P, HT, TC]), ALU.mult)\
                    .then_inc(xn_ready, 1)

            def ssm_norm(e):
                dve.wait_ge(srs_full, e + 1)
                dve.reciprocal(dtb[0:SROWS, 2], dtb[0:SROWS, 2]).then_inc(srs_inv, 1)
                dve.wait_ge(srs_inv, e + 1)
                dve.tensor_tensor(ssm[:, :], ssm[:, :], dtb[0:SROWS, 2], ALU.mult).then_inc(ssm_ready, 1)

            dve.sem_inc(product_done, NW)
            dve.sem_inc(dt_pool, 3)
            for free in (*evacuated, d_free):
                dve.sem_inc(free, 1)
            for free in (conv_done, wssm_used, dt_bank_free, unit_done):
                dve.sem_inc(free, 2)
            dve.memset(zeros[:, :], 0.0).then_inc(zeros_set, 1)
            for k in range(2):
                dve.memset(decay[:, k, :, 0:1], 0.0).then_inc(decay_free, 1)
            dve.wait_ge(aneg_exp, 1)
            dve.tensor_scalar(aneg[:, :], aneg[:, :], -1.0, None, ALU.mult).then_inc(aneg_full, 1)
            layernorm(0)
            ring = pre_ring(0)
            with dve.Fori(0, 2) as g:
                for s in range(S4):
                    convolution(0, g, s, ring, 2 * s)
            layernorm(1)
            ssm_norm(0)

            for c in range(NCH):
                more = c < NCH - 1
                for half in range(2):
                    with dve.Fori(0, 2) as g:
                        for s in range(S4):
                            scan_first(c, half, g, s, 0)
                            if more and half == 0:
                                convolution(c + 1, g, s, m_ring(c, half), m_off(c, s, 0, False))
                            scan_rest(c, half, g, s, 0)
                            if s >= 2:
                                output_add(c, half, g, s, 0)
                                output_add(c, half, g, s, 1)
                            scan_first(c, half, g, s, 1)
                            if s >= 2:
                                output_add(c, half, g, s, 2)
                                output_add(c, half, g, s, 3)
                            scan_rest(c, half, g, s, 1)
                            if c > 0 and s % 2:
                                combine(w_ring(c, half), w_off(c, s, "out"), c - 1, g, s, 4 * half)
                    if more and half == 0:
                        ssm_norm(c + 1)
                if c + 2 < NCH:
                    layernorm(c + 2)
            with dve.Fori(0, 4) as g:
                for s in (1, 3):
                    combine(last_ring, s, NCH - 1, g, s, 0)

        @block.gpsimd
        def _(pool):
            def store_input(e, half, g, s):
                for k in range(2):
                    ch = chan(g, s, k)
                    wait(pool, u_full if half == 0 else gate_full, ch + (e * DT + 1))
                    pool.dma_start(spill[ch, :, 1 + half, toks(e)], ut[:, k]).then_inc(ut_stored[k], 16)

            def dt_tile(e, g, s, k):
                ch = chan(g, s, k)
                n = ch + e * DT
                wait(pool, dt_chain, n * 4 + 4)
                pool.tensor_tensor(dtb[:, 1], dtb[:, 1], dtb[:, 2], ALU.subtract).then_inc(dt_pool, 1)
                wait(pool, dt_pool, n * 3 + 4)
                pool.tensor_tensor(dtb[:, 3], dtb[:, 3], dtb[:, 1], ALU.add).then_inc(dt_pool, 1)
                wait(pool, dt_pool, n * 3 + 5)
                wait(pool, dt_stored, n * 16 + 16)
                pool.tensor_tensor(dtb[:, 4], dtb[:, 3], dtb[:, 0], ALU.add).then_inc(dt_pool, 1)
                wait(pool, dt_pool, n * 3 + 6)
                pool.dma_start(spill[ch, :, 0, toks(e)], dtb[:, 4]).then_inc(dt_stored, 16)

            def store_bc(e):
                wait(pool, ssm_ready, e + 1)
                pool.dma_start(bc_d[:, toks(e)], ssm[R:SROWS, :]).then_inc(bc_stored, 16)

            def broadcast_bc(c, half):
                t0 = c * TC + half * TS
                wait(pool, bc_stored, 16 * (c + 1))
                wait(pool, driven, 4 * STEPS * (2 * c + half))
                pool.dma_start(bbc[:, :, :], bc_d[0:N, t0:t0 + TS].partition_broadcast(P)).then_inc(b_full, 16)
                wait(pool, weighted, STEPS * (2 * c + half))
                pool.dma_start(cbc[:, :, :], bc_d[N:2 * N, t0:t0 + TS].partition_broadcast(P)).then_inc(c_full, 16)

            def store_y(c, half, g, s, k):
                t0 = c * TC + half * TS
                wait(pool, unit_done, unit_no(c, half, g, s, k) + DONE)
                pool.dma_start(y_d[chan(g, s, k), :, t0:t0 + TS], yt[:, k]).then_inc(y_stored[k], 16)

            def load_gx(e, g, s, base):
                m = g * 2 + (base + s // 2)
                wait(pool, out_stored, (m + (HT * e + 1)) * 16)
                pool.dma_start(gx[:, 0], g_d[m, :, toks(e)]).then_inc(gx_in, 16)
                pool.dma_start(gx[:, 1], xT[m, :, toks(e)]).then_inc(gx_in, 16)

            def store_out(e, g, s, base):
                m = g * 2 + (base + s // 2)
                wait(pool, out_ready, m + (HT * e + 1))
                pool.dma_start(outT[m, :, toks(e)], gx[:, 0]).then_inc(out_stored, 16)

            def load_y(c):
                for k in range(2):
                    wait(pool, y_stored[k], 16 * (STEPS * (c + 1) + 1))
                if c > 0:
                    wait(pool, product_done, w_ring(c, 1).number(1, w_off(c, 3, "out")) + W_DONE)
                pool.dma_start(yin[:, :, :], y_d[:, :, toks(c)].rearrange("k p t -> p k t")).then_inc(y_in, 16)

            for buf, stored in ((ut[:, 0], ut_stored[0]), (ut[:, 1], ut_stored[1]), (dtb[:, 4], dt_stored),
                                (yt[:, 0], y_stored[0]), (yt[:, 1], y_stored[1]), (gx[:, 0], out_stored)):
                pool.dma_start(buf[:, 0:2], params[:, 0:2]).then_inc(stored, 16)
            pool.memset(facc[:, :, :], 0.0).then_inc(facc_zero, 1)
            for half in range(2):
                with pool.Fori(0, 2) as g:
                    for s in range(S4):
                        if half == 1:
                            dt_tile(0, g, s, 0)
                        store_input(0, half, g, s)
                        if half == 1:
                            dt_tile(0, g, s, 1)
                if half == 0:
                    store_bc(0)
                    broadcast_bc(0, 0)

            for c in range(NCH):
                more = c < NCH - 1
                for half in range(2):
                    with pool.Fori(0, 2) as g:
                        for s in range(S4):
                            if c > 0 and s % 2 == 0:
                                load_gx(c - 1, g, s, 4 * half)
                            store_y(c, half, g, s, 0)
                            if more:
                                store_input(c + 1, half, g, s)
                            if more and half == 1:
                                dt_tile(c + 1, g, s, 0)
                            store_y(c, half, g, s, 1)
                            if more and half == 1:
                                dt_tile(c + 1, g, s, 1)
                            if c > 0 and s % 2:
                                store_out(c - 1, g, s, 4 * half)
                    if half == 0:
                        broadcast_bc(c, 1)
                        if more:
                            store_bc(c + 1)
                if more:
                    broadcast_bc(c + 1, 0)
                load_y(c)
                wait(pool, g_full, c + 1)
                pool.dma_start(g_d[:, :, toks(c)].rearrange("m p t -> p m t"), facc[:, :, :]).then_inc(g_stored, 16)
                wait(pool, g_stored, 16 * (c + 1))
                if more:
                    pool.memset(facc[:, :, :], 0.0).then_inc(facc_zero, 1)
            with pool.Fori(0, 4) as g:
                for s in range(0, S4, 2):
                    load_gx(NCH - 1, g, s, 0)
                    store_out(NCH - 1, g, s, 0)
            wait(pool, out_stored, 16 * (HT * NCH + 1))


def kernel(**inputs):
    import numpy as np
    import concourse.bacc as bacc
    from concourse.bass_utils import run_bass_kernel_spmd

    def arr(name):
        return np.asarray(inputs[name])

    def tiles(w):
        k, m = w.shape
        w = w.reshape(k // H, 8, P, m // P, P).transpose(3, 0, 2, 1, 4)
        return np.ascontiguousarray(w).reshape(m // P, k // H, P, 8 * P)

    def channels(v, n):
        return v.reshape(-1, P, n).transpose(1, 0, 2).reshape(P, -1)

    x = arr("L0_attn_hidden_states")
    w_in = arr("L0_attn_W_in").T
    blk = np.zeros((P, SROWS), np.float32)
    for a, n in ((0, R), (R, N), (R + N, N)):
        blk[a:a + n, a:a + n] = 1.0 / n
    consts = np.zeros((P, NPAR - C_ONES), np.float32)
    consts[:, 0:P] = 1.0 / H
    consts[:, C_BLK - C_ONES:C_BLK - C_ONES + SROWS] = blk
    consts[:, C_EPS - C_ONES] = LN_EPS
    consts[:, C_EPS - C_ONES + 1] = RMS_EPS
    params = np.concatenate([
        channels(arr("L0_attn_conv_w"), K), channels(arr("L0_attn_conv_b"), 1), channels(arr("L0_attn_b_dt"), 1),
        channels(arr("L0_attn_D"), 1), channels(arr("L0_attn_A_log"), N), channels(arr("L0_ffn_inter_b"), 1),
        channels(arr("L0_ffn_output_b"), 1), consts], axis=1)
    arrays = {
        "xT": np.ascontiguousarray(x.reshape(T, H).T).reshape(HT, P, T),
        "params": np.ascontiguousarray(params),
        "w_x": tiles(w_in[:, :D_IN])[:, 0],
        "w_g": tiles(w_in[:, D_IN:])[:, 0],
        "w_1": tiles(arr("L0_ffn_inter_w"))[:, 0],
        "w_2": np.ascontiguousarray(tiles(arr("L0_ffn_output_w")).transpose(1, 0, 2, 3)).reshape(FT, P, 8 * P),
        "w_o": tiles(arr("L0_attn_W_out").T).reshape(DT, P, 8 * P),
        "w_ssm": np.ascontiguousarray(arr("L0_attn_W_x").T).reshape(DT, P, SROWS),
        "w_dt": np.ascontiguousarray(arr("L0_attn_W_dt").reshape(DT, P, R).transpose(0, 2, 1)),
    }
    nc = bacc.Bacc("TRN2", target_bir_lowering=False, num_devices=1)
    args = {}
    maps = {}
    for name, a in arrays.items():
        maps[f"in_{name}"] = np.ascontiguousarray(a)
        args[name] = nc.dram_tensor(f"in_{name}", a.shape, mybir.dt.from_np(a.dtype), kind="ExternalInput").ap()
    args["outT"] = nc.dram_tensor("out_0", (HT, P, T), F32, kind="ExternalOutput").ap()
    build(nc, **args)
    r = run_bass_kernel_spmd(nc, [maps], core_ids=[0])
    got = r.results[0]["out_0"]
    return np.ascontiguousarray(np.asarray(got).reshape(H, T).T).reshape(B, L, H)
```

```python
from contextlib import ExitStack

import concourse.bass as bass
from concourse import mybir

F32 = mybir.dt.float32
ALU = mybir.AluOpType
ACT = mybir.ActivationFunctionType
AX = mybir.AxisListType

P = 128
H = 1024
D_IN = 2048
N = 16
K = 4
R = 64
F = 4096
B, L = 2, 1024
T = B * L
LN_EPS, RMS_EPS = 1e-5, 1e-6

TC = 512
NCH = T // TC
CPB = L // TC
HT = H // P
DT = D_IN // P
FT = F // P
GRP = 8
STEPS = 16
S4 = 4
TS = 256
Q = 4
NQ = N // Q
SROWS = R + 2 * N
NW = 4
NM = 4

C_CONVW = 0
C_CONVB = C_CONVW + DT * K
C_BDT = C_CONVB + DT
C_D = C_BDT + DT
C_ALOG = C_D + DT
C_B1 = C_ALOG + DT * N
C_B2 = C_B1 + FT
C_ONES = C_B2 + HT
C_BLK = C_ONES + P
C_EPS = C_BLK + SROWS
NPAR = C_EPS + 2


def step_tiles(c, half, s):
    ins, ffn = [("in", k) for k in range(2)], [("ffn", k) for k in range(4)]
    if c == NCH - 1:
        tiles = ffn[:2] + ([("early", 0), ("early", 1)] if half == 1 else []) + ffn[2:]
    else:
        tiles = ffn[:2] + ins + ffn[2:] if s == 0 else ins + ffn
    return tiles + ([("out", 0)] if c > 0 else [])


def w_per_step(c, half):
    return len(step_tiles(c, half, 0))


def m_per_step(c):
    return 4 + (2 if c < NCH - 1 else 0)


PRE_TILES = 2 * DT
W_BASE = [PRE_TILES + STEPS // 2 * sum(w_per_step(b, h) for b in range(c) for h in range(2)) for c in range(NCH + 1)]
M_BASE = [PRE_TILES + STEPS * sum(m_per_step(b) for b in range(c)) for c in range(NCH + 1)]
assert all(b % NW == 0 for b in W_BASE) and all(b % NM == 0 for b in M_BASE)


class Ring:

    def __init__(self, base, per, n):
        self.base, self.per, self.n = base, per, n

    def slot(self, off):
        return off % self.n

    def turn(self, g, off):
        return g * (self.per * S4 // self.n) + (self.base // self.n + off // self.n)

    def number(self, g, off):
        return g * (self.per * S4) + (self.base + off)


def build(nc, xT, params, w_x, w_g, w_1, w_2, w_o, w_ssm, w_dt, outT):
    spill = nc.dram_tensor("spill", (DT, P, 3, T), F32, kind="Internal").ap()
    y_d = nc.dram_tensor("y_d", (DT, P, T), F32, kind="Internal").ap()
    g_d = nc.dram_tensor("g_d", (HT, P, T), F32, kind="Internal").ap()
    bc_d = nc.dram_tensor("bc_d", (2 * N, T), F32, kind="Internal").ap()

    ctx = ExitStack()
    with ctx:
        def sb(name, shape):
            return ctx.enter_context(nc.sbuf_tensor(name, shape, F32))

        def ps(name):
            return ctx.enter_context(nc.psum_tensor(name, [P, TC], F32))

        def sem(name):
            return ctx.enter_context(nc.semaphore(name))

        def sems(name, n):
            return [sem(f"{name}{i}") for i in range(n)]

        par = sb("par", [P, NPAR])
        xn = [sb(f"xn{i}", [P, HT, TC]) for i in range(2)]
        wts = sb("wts", [P, NW, 8, P])
        hid = sb("hid", [P, GRP, TC])
        facc = sb("facc", [P, HT, TC])
        yin = sb("yin", [P, DT, TC])
        bbc = sb("bbc", [P, N, TS])
        cbc = sb("cbc", [P, N, TS])
        work = sb("work", [P, N, TS + 1])
        decay = sb("decay", [P, 2, Q, TS + 1])
        unit = sb("unit", [P, 2, 3, TS])
        dtu = sb("dtu", [P, TS])
        yt = sb("yt", [P, 2, TS])
        xin = sb("xin", [P, 2, K - 1 + TC])
        ut = sb("ut", [P, 2, TC])
        dtb = sb("dtb", [P, 5, TC])
        ssm = sb("ssm", [SROWS, TC])
        gx = sb("gx", [P, 2, TC])
        wssm = sb("wssm", [P, 2, SROWS])
        wdt = sb("wdt", [R, 2, P])
        aneg = sb("aneg", [P, DT * N])
        carry = sb("carry", [P, DT, N])
        halo = sb("halo", [P, DT, K - 1])
        zeros = sb("zeros", [P, K])

        pm = [ps(f"pm{i}") for i in range(NM)]
        p_out, p_ssm = ps("p_out"), ps("p_ssm")
        p_st = [ps("p_st0"), ps("p_st1")]

        pre_wssm = hid[:, :, :].rearrange("p k t -> p (k t)")[:, 0:2 * S4 * SROWS].rearrange("p (n m) -> p n m", m=SROWS)
        y_early = xn[NCH % 2][:, :, :].rearrange("p k t -> p (k t)").rearrange("p (d t) -> p d t", t=TS)
        early = dtb[:, 0:4].rearrange("p b t -> p (b t)").rearrange("p (m t) -> p m t", t=TS)
        resid = xn[(NCH - 1) % 2][:, :, :]
        p_last = [p_ssm, *pm[0:3], *p_st, pm[3], p_out]

        params_in, zeros_set, aneg_exp, aneg_full = sem("params_in"), sem("zeros_set"), sem("aneg_exp"), sem("aneg_full")
        w_full, product_done, evacuated = sems("w_full", NW), sem("product_done"), sems("evacuated", NM)
        x_in, mean_full, centered = sems("x_in", 2), sem("mean_full"), sem("centered")
        sq_full, sq_used, var_full, std_full = sem("sq_full"), sem("sq_used"), sem("var_full"), sem("std_full")
        rstd_full, xn_ready = sem("rstd_full"), sem("xn_ready")
        conv_tap, conv_done = sem("conv_tap"), sem("conv_done")
        u_full, gate_full, ut_stored = sem("u_full"), sem("gate_full"), sems("ut_stored", 2)
        wssm_full, wssm_used, wdt_full = sems("wssm_full", 2), sem("wssm_used"), sems("wdt_full", 2)
        ssm_full, ssm_evac, ssq_full, ms_full = sem("ssm_full"), sem("ssm_evac"), sem("ssq_full"), sem("ms_full")
        srs_full, srs_inv, ssm_ready, bc_stored = sem("srs_full"), sem("srs_inv"), sem("ssm_ready"), sem("bc_stored")
        dt_full, dt_bank_free, dt_chain = sem("dt_full"), sem("dt_bank_free"), sem("dt_chain")
        dt_sum, dt_stored = sem("dt_sum"), sem("dt_stored")
        b_full, c_full, unit_in = sem("b_full"), sem("c_full"), sems("unit_in", 2)
        decay_full, decay_free = sem("decay_full"), sem("decay_free")
        dtu_full, driven, carried, weighted = sem("dtu_full"), sem("driven"), sem("carried"), sem("weighted")
        summed, skipped, unit_done, y_stored = sem("summed"), sem("skipped"), sem("unit_done"), sems("y_stored", 2)
        h_full, facc_zero, g_full, g_stored = sem("h_full"), sem("facc_zero"), sem("g_full"), sem("g_stored")
        y_in, d_full, d_free = sem("y_in"), sem("d_full"), sem("d_free")
        gx_in, out_ready, out_stored = sem("gx_in"), sem("out_ready"), sem("out_stored")

        y_early_in, y_last_in, last_free, resid_in = sem("y_early_in"), sems("y_last_in", 2), sem("last_free"), sem("resid_in")
        early_full, early_ready, last_ready, last_stored = sem("early_full"), sem("early_ready"), sem("last_ready"), sem("last_stored")
        pre_wssm_full, pre_chain, pre_exp, pre_ln = sem("pre_wssm_full"), sem("pre_chain"), sem("pre_exp"), sem("pre_ln")
        pre_stored = sems("pre_stored", 2)
        last_scaled = sem("last_scaled")
        waits_met = sem("waits_met")

        DONE = 3
        W_DONE = NW + 1

        def col(base, i=0, n=1):
            return par[:, base + i:base + i + n]

        def toks(e):
            return slice(e * TC, (e + 1) * TC)

        def chan(g, s, k):
            return g * (2 * S4) + (2 * s + k)

        def unit_no(c, half, g, s, k):
            return g * (2 * S4) + (c * 2 * STEPS + half * STEPS + 2 * s + k)

        def turn2(e, g, s, per=8, base=0):
            return g * S4 + (e * per + base + s)

        def m_off(c, s, kind, k=0):
            return s * m_per_step(c) + [t for t in step_tiles(c, 0, s) if t[0] != "out"].index((kind, k))

        def w_off(c, half, s, kind, k=0):
            return s * w_per_step(c, half) + step_tiles(c, half, s).index((kind, k))

        def w_ring(c, half):
            return Ring(W_BASE[c] + half * 8 * w_per_step(c, 0), w_per_step(c, half), NW)

        def m_ring(c, half):
            return Ring(M_BASE[c] + half * 8 * m_per_step(c), m_per_step(c), NM)

        def pre_ring(half):
            return Ring(half * DT, 2, NW)

        last_ring = Ring(W_BASE[NCH], 1, NW)

        def wait(eng, semaphore, count):
            eng.wait_ge(semaphore, count)
            if not isinstance(count, int):
                eng.sem_inc(waits_met, 1)

        def broadcast_b(eng, c, half):
            t0 = c * TC + half * TS
            eng.wait_ge(bc_stored, 16 * (c + 1))
            if c + half > 0:
                eng.wait_ge(driven, 4 * STEPS * (2 * c + half))
            eng.dma_start(bbc[:, :, :], bc_d[0:N, t0:t0 + TS].partition_broadcast(P)).then_inc(b_full, 16)

        def broadcast_c(eng, c, half):
            t0 = c * TC + half * TS
            if c + half > 0:
                eng.wait_ge(weighted, STEPS * (2 * c + half))
            eng.dma_start(cbc[:, :, :], bc_d[N:2 * N, t0:t0 + TS].partition_broadcast(P)).then_inc(c_full, 16)

        def pre_dt(s):
            return [yin[:, 8 * (s % 2) + 2 * i:8 * (s % 2) + 2 * i + 2] for i in range(4)]

        block = ctx.enter_context(nc.Block())

        @block.sync
        def _(sp):
            def weight(ring, g, off, src):
                slot = ring.slot(off)
                wait(sp, product_done, ring.number(g, off) + 1)
                sp.dma_start(wts[:, slot].rearrange("p k m -> p (k m)"), src).then_inc(w_full[slot], 16)

            def ssm_weights(e, g, s):
                for k in range(2):
                    wait(sp, wssm_used, chan(g, s, k) + (e * DT + 1))
                    sp.dma_start(wssm[:, k], w_ssm[chan(g, s, k)]).then_inc(wssm_full[k], 16)

            def dt_weights(e, g, s):
                for k in range(2):
                    wait(sp, dt_bank_free, chan(g, s, k) + (e * DT + 1))
                    sp.dma_start(wdt[:, k], w_dt[chan(g, s, k)]).then_inc(wdt_full[k], 16)

            def x_chunk(e):
                sp.dma_start(xn[e % 2][:, :, :], xT[:, :, toks(e)].rearrange("k p t -> p k t")).then_inc(x_in[e % 2], 16)

            def scan_unit(c, half, g, s, k):
                wait(sp, unit_done, unit_no(c, half, g, s, k) + 1)
                if half == 0:
                    wait(sp, ut_stored[k], 16 * (turn2(c, g, s, 16, 8) + 2))
                    if c == 0:
                        wait(sp, pre_stored[s % 2], g * 64 + (16 + 32 * (s // 2 + 1)))
                    else:
                        wait(sp, dt_stored, 16 * (chan(g, s, k) + ((c - 1) * DT + 2)))
                t0 = c * TC + half * TS
                sp.dma_start(unit[:, k], spill[chan(g, s, k), :, :, t0:t0 + TS]).then_inc(unit_in[k], 16)

            def load_y_last(j):
                c = NCH - 1
                wait(sp, product_done, w_ring(c, 1).number(1, w_off(c, 1, 2 + j, "out")) + W_DONE)
                for k in range(2):
                    wait(sp, y_stored[k], 16 * (STEPS * c + 8 + 4 * (j + 1) + 1))
                sp.dma_start(yin[:, 8 * j:8 * j + 8, 0:TS],
                             y_d[8 * j:8 * j + 8, :, T - TS:T].rearrange("k p t -> p k t")).then_inc(y_last_in[j], 16)

            sp.dma_start(par[:, :], params).then_inc(params_in, 16)
            x_chunk(0)
            x_chunk(1)
            sp.dma_start(pre_wssm, w_ssm[0:2 * S4].rearrange("n p m -> p n m")).then_inc(pre_wssm_full, 16)
            ring = pre_ring(0)
            for g in range(2):
                for s in range(S4):
                    for k in range(2):
                        weight(ring, g, 2 * s + k, w_x[chan(g, s, k)])
                    if g == 1 and s == 0:
                        sp.wait_ge(wssm_used, 2 * S4 + 2)
                        sp.dma_start(pre_wssm, w_ssm[2 * S4:].rearrange("n p m -> p n m")).then_inc(pre_wssm_full, 16)
            ring = pre_ring(1)
            with sp.Fori(0, 2) as g:
                for s in range(S4):
                    for k in range(2):
                        weight(ring, g, 2 * s + k, w_g[chan(g, s, k)])
                    dt_weights(0, g, s)
            broadcast_b(sp, 0, 0)
            broadcast_c(sp, 0, 0)

            for c in range(NCH):
                for half in range(2):
                    ring = w_ring(c, half)
                    with sp.Fori(0, 2) as g:
                        for s in range(S4):
                            for kind, k in step_tiles(c, half, s):
                                src = {"in": (w_x if half == 0 else w_g, chan(g, s, k)),
                                       "ffn": (w_1 if s < 2 else w_2, g * GRP + (2 * half * GRP + 4 * (s % 2) + k)),
                                       "early": (w_o, g * (2 * S4) + (2 * s + k)),
                                       "out": (w_o, g * S4 + (2 * half * S4 + s))}[kind]
                                weight(ring, g, w_off(c, half, s, kind, k), src[0][src[1]])
                                if (kind, k) == ("ffn", 0):
                                    scan_unit(c, half, g, s, 0)
                                if (kind, k) == ("ffn", 3):
                                    scan_unit(c, half, g, s, 1)
                                if c < NCH - 1 and half == 0 and (kind, k) == ("ffn", 1):
                                    ssm_weights(c + 1, g, s)
                                if half == 1 and (kind, k) == ("in", 1):
                                    dt_weights(c + 1, g, s)
                if c + 2 < NCH:
                    wait(sp, product_done, w_ring(c, 1).number(1, w_off(c, 1, 1, "ffn", 3)) + W_DONE)
                    x_chunk(c + 2)
            load_y_last(0)
            wait(sp, product_done, w_ring(NCH - 1, 1).number(1, w_off(NCH - 1, 1, 1, "ffn", 3)) + W_DONE)
            sp.dma_start(resid, xT[:, :, toks(NCH - 1)].rearrange("k p t -> p k t")).then_inc(resid_in, 16)
            for i in range(2 * HT):
                if i == 6:
                    load_y_last(1)
                weight(last_ring, 0, i, w_o[2 * (i % HT) + i // HT])
            sp.wait_ge(early_ready, 1)
            sp.dma_start(outT[:, :, T - TC:T - TS].rearrange("m p t -> p m t"), early).then_inc(last_stored, 16)
            for m in range(HT):
                sp.wait_ge(last_ready, m + 1)
                sp.dma_start(outT[m, :, T - TS:T], facc[:, m, TS:]).then_inc(last_stored, 16)
            sp.wait_ge(last_stored, 16 * (HT + 1))

        @block.tensor
        def _(pe):
            def product(out, ring, g, off, rhs, start=True, stop=True):
                slot = ring.slot(off)
                pe.wait_ge(w_full[slot], 16 * (ring.turn(g, off) + 1))
                for k in range(8):
                    mm = pe.matmul(out, lhsT=wts[:, slot, k], rhs=rhs[:, k],
                                   start=start and k == 0, stop=stop and k == 7)
                mm.then_inc(product_done, 1)

            def ring_product(wring, mring, g, woff, moff, rhs):
                b = mring.slot(moff)
                pe.wait_ge(evacuated[b], mring.turn(g, moff) + 1)
                product(pm[b][:, :], wring, g, woff, rhs)

            def out_product(wring, g, woff, e, s, base=0):
                if s % 2 == 0:
                    pe.wait_ge(y_in, 16 * (e + 1))
                    pe.wait_ge(d_free, g * 2 + (HT * e + base + s // 2 + 1))
                product(p_out[:, :], wring, g, woff, yin[:, 8 * (s % 2):8 * (s % 2) + 8],
                        start=s % 2 == 0, stop=s % 2 == 1)

            def last_product(wring, g, woff, s, j, rhs, n):
                if j == 0:
                    pe.wait_ge(last_free, n + 1)
                product(p_st[s % 2][:, 0:TS], wring, g, woff, rhs, start=j == 0, stop=j == 1)

            def mean_sum(e):
                pe.wait_ge(x_in[e % 2], 16 * (e // 2 + 1))
                if e > 0:
                    pe.wait_ge(centered, HT * e)
                for k in range(HT):
                    mm = pe.matmul(p_st[0][:, :], lhsT=col(C_ONES, 0, P), rhs=xn[e % 2][:, k],
                                   start=k == 0, stop=k == HT - 1)
                mm.then_inc(mean_full, 1)

            def square_sum(e):
                for k in range(HT):
                    pe.wait_ge(sq_full, HT * e + k + 1)
                    pe.matmul(p_st[1][:, :], lhsT=col(C_ONES, 0, P), rhs=dtb[:, k % 2],
                              start=k == 0, stop=k == HT - 1).then_inc(sq_used, 1)

            def ssm_open(e):
                if e == 0:
                    pe.wait_ge(zeros_set, 1)
                if e > 0:
                    pe.wait_ge(srs_full, e)
                pe.matmul(p_ssm[0:SROWS, :], lhsT=col(C_BLK, 0, SROWS), rhs=zeros[:, 0:1].to_broadcast([P, TC]), start=True, stop=False,
                          skip_group_check=True)

            def ssm_close(e):
                pe.matmul(p_ssm[0:SROWS, :], lhsT=col(C_BLK, 0, SROWS), rhs=zeros[:, 0:1].to_broadcast([P, TC]), start=False, stop=True,
                          skip_group_check=True).then_inc(ssm_full, 1)

            def ssm_products(e, g, s):
                for k in range(2):
                    if e == 0:
                        pe.wait_ge(pre_wssm_full, g * 16 + 16)
                    else:
                        pe.wait_ge(wssm_full[k], 16 * (turn2(e - 1, g, s) + 1))
                    pe.wait_ge(u_full, chan(g, s, k) + (e * DT + 1))
                    pe.matmul(p_ssm[0:SROWS, :], lhsT=pre_wssm[:, 2 * s + k] if e == 0 else wssm[:, k], rhs=ut[:, k], start=False, stop=False,
                              skip_group_check=True).then_inc(wssm_used, 1)

            def ssm_square_means(e):
                pe.wait_ge(ssq_full, e + 1)
                pe.matmul(p_ssm[0:SROWS, :], lhsT=par[0:SROWS, C_BLK:C_BLK + SROWS],
                          rhs=dtb[0:SROWS, 3], start=True, stop=True).then_inc(ms_full, 1)

            def dt_product(e, g, s, k):
                n = chan(g, s, k) + e * DT
                pe.wait_ge(wdt_full[k], 16 * (turn2(e, g, s) + 1))
                pe.wait_ge(ssm_ready, e + 1)
                pe.wait_ge(dt_bank_free, n + 1)
                pe.matmul(p_st[k][:, :], lhsT=wdt[:, k], rhs=ssm[0:R, :], start=True, stop=True)\
                    .then_inc(dt_full, 1)

            pe.wait_ge(params_in, 16)
            mean_sum(0)
            square_sum(0)
            mean_sum(1)
            pe.wait_ge(xn_ready, 1)
            ssm_open(0)
            ring = pre_ring(0)
            with pe.Fori(0, 2) as g:
                for s in range(S4):
                    for k in range(2):
                        ring_product(ring, ring, g, 2 * s + k, 2 * s + k, xn[0])
                    if s > 0:
                        ssm_products(0, g, s - 1)
                ssm_products(0, g, S4 - 1)
            square_sum(1)
            ssm_close(0)
            ssm_square_means(0)
            ring = pre_ring(1)
            with pe.Fori(0, 2) as g:
                for s in range(S4):
                    for k in range(2):
                        ring_product(ring, ring, g, 2 * s + k, 2 * s + k, xn[0])
                    dt_product(0, g, s, 0)
                    dt_product(0, g, s, 1)

            for c in range(NCH):
                more = c < NCH - 1
                if more:
                    ssm_open(c + 1)
                for half in range(2):
                    if not more and half == 1:
                        pe.wait_ge(dt_bank_free, 2 + DT * NCH)
                    wring, mring = w_ring(c, half), m_ring(c, half)
                    with pe.Fori(0, 2) as g:
                        for s in range(S4):
                            for kind, k in step_tiles(c, half, s):
                                woff = w_off(c, half, s, kind, k)
                                if kind == "in":
                                    if s == 0:
                                        pe.wait_ge(xn_ready, c + 2)
                                    ring_product(wring, mring, g, woff, m_off(c, s, "in", k), xn[(c + 1) % 2])
                                elif kind == "ffn":
                                    if s == 2 and k == 0:
                                        pe.wait_ge(h_full, g * 2 + (c * 8 + half * 4 + 2))
                                    ring_product(wring, mring, g, woff, m_off(c, s, "ffn", k), xn[c % 2] if s < 2 else hid)
                                elif kind == "early":
                                    pe.wait_ge(y_early_in, 16)
                                    last_product(wring, g, woff, s, k, y_early[:, 8 * k:8 * k + 8], g * S4 + s)
                                else:
                                    if more and half == 0:
                                        ssm_products(c + 1, g, s)
                                    out_product(wring, g, woff, c - 1, s, 4 * half)
                                if more and half == 1 and (kind, k) == ("in", 1):
                                    dt_product(c + 1, g, s, 0)
                                if more and half == 1 and (kind, k) == ("ffn", 2 if s == 0 else 1):
                                    dt_product(c + 1, g, s, 1)
                            if c == 0 and half == 0:
                                ssm_products(c + 1, g, s)
                    if c < NCH - 1 and half == 0:
                        ssm_close(c + 1)
                        ssm_square_means(c + 1)
                if c + 2 < NCH:
                    pe.wait_ge(dt_bank_free, 2 + DT * (c + 2))
                    mean_sum(c + 2)
                    square_sum(c + 2)
            for i in range(2 * HT):
                j, m = i // HT, i % HT
                if i == 0:
                    for bank in evacuated:
                        pe.wait_ge(bank, M_BASE[NCH] // NM + 1)
                if i == 4:
                    pe.wait_ge(last_free, HT + 2)
                if i == HT - 1:
                    pe.wait_ge(d_free, HT * (NCH - 1) + 1)
                if m == 0:
                    pe.wait_ge(y_last_in[j], 16)
                product(p_last[m][:, 0:TS], last_ring, 0, i, yin[:, 8 * j:8 * j + 8, 0:TS], start=j == 0, stop=j == 1)

        @block.scalar
        def _(act):
            def decays(c, half, g, s, k, quarters):
                U = unit_no(c, half, g, s, k)
                if quarters[0] == 0:
                    act.wait_ge(unit_in[k], 16 * (turn2(c, g, s, STEPS, 8 * half) + 1))
                for q in quarters:
                    act.wait_ge(decay_free, U * 4 + (q + 1))
                    for i in range(Q):
                        a = chan(g, s, k) * N + (q * Q + i)
                        ins = act.activation(decay[:, q % 2, i, 1:], unit[:, k, 0], ACT.Exp, scale=aneg[:, bass.ds(a, 1)])
                    ins.then_inc(decay_full, 1)

            def input_tile(e, half, g, s, k, wring, woff, mring, moff):
                b = mring.slot(moff)
                ch = chan(g, s, k)
                act.wait_ge(product_done, wring.number(g, woff) + W_DONE)
                if half == 0:
                    act.wait_ge(conv_done, ch + (e * DT + 1))
                    first = e % CPB == 0
                    act.activation(xin[:, k, 0:K - 1], zeros[:, 0:K - 1] if first else halo[:, ch], ACT.Copy)
                    if first:
                        act.activation(halo[:, ch], pm[b][:, TC - K + 1:TC], ACT.Copy)
                    act.activation(xin[:, k, K - 1:], pm[b][:, :], ACT.Copy).then_inc(evacuated[b], 1)
                else:
                    act.wait_ge(ut_stored[k], 16 * (turn2(e, g, s, 16, 8) + 1))
                    act.activation(ut[:, k], pm[b][:, :], ACT.Copy).then_inc(evacuated[b], 1)

            def input_silu(e, half, g, s, mring, *moffs):
                for k in range(2):
                    ch = chan(g, s, k)
                    if half == 0:
                        act.wait_ge(conv_done, ch + (e * DT + DONE))
                        act.activation(ut[:, k], ut[:, k], ACT.Silu, bias=par[:, bass.ds(ch + C_CONVB, 1)])\
                            .then_inc(u_full, 1)
                    else:
                        act.wait_ge(evacuated[mring.slot(moffs[k])], mring.turn(g, moffs[k]) + 2)
                        act.activation(ut[:, k], ut[:, k], ACT.Silu).then_inc(gate_full, 1)

            def hidden_tile(c, half, g, s, k):
                wring, mring = w_ring(c, half), m_ring(c, half)
                b = mring.slot(m_off(c, s, "ffn", k))
                act.wait_ge(product_done, wring.number(g, w_off(c, half, s, "ffn", k)) + W_DONE)
                act.activation(hid[:, 4 * s + k], pm[b][:, :], ACT.Identity,
                               bias=par[:, bass.ds(g * GRP + (C_B1 + 2 * half * GRP + 4 * s + k), 1)])\
                    .then_inc(evacuated[b], 1)

            def hidden_gelu(c, half, g, s):
                hidden_tile(c, half, g, s, 2)
                hidden_tile(c, half, g, s, 3)
                mring, moff = m_ring(c, half), m_off(c, s, "ffn", 3)
                act.wait_ge(evacuated[mring.slot(moff)], mring.turn(g, moff) + 2)
                act.activation(hid[:, 4 * s:4 * s + 4], hid[:, 4 * s:4 * s + 4], ACT.Gelu_apprx_tanh)\
                    .then_inc(h_full, 1)

            def dt_tile(e, g, s, k):
                ch = chan(g, s, k)
                n = ch + (e - 1) * DT
                bias = par[:, bass.ds(ch + C_BDT, 1)]
                act.wait_ge(xn_ready, 2)
                act.wait_ge(dt_full, n + (DT + 1))
                act.wait_ge(dt_sum, n * 3 + 3)
                act.activation(dtb[:, 0], p_st[k][:, :], ACT.Relu, bias=bias)
                act.activation(dtb[:, 1], p_st[k][:, :], ACT.Abs, bias=bias).then_inc(dt_bank_free, 1)
                act.wait_ge(dt_bank_free, n + (DT + DONE))
                act.activation(dtb[:, 1], dtb[:, 1], ACT.Exp, scale=-1.0).then_inc(dt_chain, 1)
                act.wait_ge(dt_chain, n * 3 + 1)
                act.activation(dtb[:, 2], dtb[:, 1], ACT.Identity, bias=1.0).then_inc(dt_chain, 1)
                act.wait_ge(dt_chain, n * 3 + 2)
                act.activation(dtb[:, 3], dtb[:, 2], ACT.Ln).then_inc(dt_chain, 1)

            def pre_dt_logs(g, s):
                minus_abs, _, p, w = pre_dt(s)
                act.wait_ge(pre_chain, g * 24 + (6 * s + 2))
                act.activation(p, minus_abs, ACT.Exp).then_inc(pre_exp, 1)
                act.wait_ge(pre_chain, g * 24 + (6 * s + 3))
                act.activation(minus_abs, w, ACT.Ln).then_inc(pre_ln, 1)

            def ssm_squares(e):
                act.wait_ge(ssm_full, e + 1)
                if e > 0:
                    act.wait_ge(bc_stored, 16 * e)
                if e > 1:
                    act.wait_ge(dt_sum, 3 * (DT * (e - 1) + 1))
                act.activation(ssm[:, :], p_ssm[0:SROWS, :], ACT.Copy).then_inc(ssm_evac, 1)
                act.wait_ge(ssm_evac, e + 1)
                act.activation(dtb[0:SROWS, 3], ssm[:, :], ACT.Square).then_inc(ssq_full, 1)

            def ssm_root(e):
                act.wait_ge(ms_full, e + 1)
                act.activation(dtb[0:SROWS, 3], p_ssm[0:SROWS, :], ACT.Sqrt, bias=par[0:SROWS, C_EPS + 1:C_EPS + 2])\
                    .then_inc(srs_full, 1)
                act.wait_ge(ssm_ready, e + 1)

            def layernorm(e):
                if e >= 2:
                    act.wait_ge(dt_sum, 3 * (DT * (e - 1) + 1))
                for k in range(HT):
                    if k >= 2:
                        act.wait_ge(sq_used, HT * e + k - 1)
                    act.wait_ge(centered, HT * e + k + 1)
                    act.activation(dtb[:, k % 2], xn[e % 2][:, k], ACT.Square).then_inc(sq_full, 1)
                act.wait_ge(sq_used, HT * (e + 1))
                act.activation(dtb[:, 2], p_st[1][:, :], ACT.Sqrt, bias=col(C_EPS)).then_inc(std_full, 1)

            def early_tile(g, s):
                c, half = NCH - 1, 1
                act.wait_ge(product_done, w_ring(c, half).number(g, w_off(c, half, s, "early", 1)) + W_DONE)
                act.activation(early[:, bass.ds(g * S4 + s, 1)], p_st[s % 2][:, 0:TS].unsqueeze(1), ACT.Copy)\
                    .then_inc(last_free, 1)

            act.wait_ge(params_in, 16)
            act.activation(aneg[:, :], col(C_ALOG, 0, DT * N), ACT.Exp).then_inc(aneg_exp, 1)
            layernorm(0)
            act.wait_ge(zeros_set, 1)
            for half in range(2):
                ring = pre_ring(half)
                with act.Fori(0, 2) as g:
                    for s in range(S4):
                        for k in range(2):
                            input_tile(0, half, g, s, k, ring, 2 * s + k, ring, 2 * s + k)
                        input_silu(0, half, g, s, ring, 2 * s, 2 * s + 1)
                        if half == 1:
                            pre_dt_logs(g, s)
                if half == 0:
                    layernorm(1)
                    ssm_squares(0)
                    ssm_root(0)
            act.wait_ge(aneg_full, 1)

            for c in range(NCH):
                more = c < NCH - 1
                for half in range(2):
                    wring, mring = w_ring(c, half), m_ring(c, half)
                    with act.Fori(0, 2) as g:
                        for s in range(S4):
                            def input_of_next(k):
                                input_tile(c + 1, half, g, s, k, wring, w_off(c, half, s, "in", k), mring, m_off(c, s, "in", k))

                            decays(c, half, g, s, 0, (0, 1))
                            if s in (1, 2):
                                hidden_gelu(c, half, g, s - 1)
                            decays(c, half, g, s, 0, (2, 3))
                            if s == 0:
                                hidden_tile(c, half, g, s, 0)
                                hidden_tile(c, half, g, s, 1)
                                decays(c, half, g, s, 1, (0, 1))
                                if more:
                                    input_of_next(0)
                                decays(c, half, g, s, 1, (2, 3))
                                if more:
                                    input_of_next(1)
                                    input_silu(c + 1, half, g, s, mring, m_off(c, s, "in", 0), m_off(c, s, "in", 1))
                                    if half == 1:
                                        dt_tile(c + 1, g, s, 0)
                            else:
                                if more:
                                    input_of_next(0)
                                    input_of_next(1)
                                    if half == 1:
                                        dt_tile(c + 1, g, s, 0)
                                decays(c, half, g, s, 1, (0, 1))
                                if s == 1:
                                    hidden_tile(c, half, g, s, 0)
                                decays(c, half, g, s, 1, (2, 3))
                                if more:
                                    input_silu(c + 1, half, g, s, mring, m_off(c, s, "in", 0), m_off(c, s, "in", 1))
                                if s == 1:
                                    hidden_tile(c, half, g, s, 1)
                            if more and half == 1:
                                dt_tile(c + 1, g, s, 1)
                            if c == NCH - 1 and half == 1:
                                early_tile(g, s)
                    if more and half == 0:
                        ssm_squares(c + 1)
                    if half == 0 or more:
                        broadcast_b(act, c + half, 1 - half)
                    if more and half == 0:
                        ssm_root(c + 1)
                    if half == 0 or more:
                        broadcast_c(act, c + half, 1 - half)
                if c + 2 < NCH:
                    layernorm(c + 2)
                if c == NCH - 2:
                    act.wait_ge(dt_sum, 3 * (DT * (NCH - 1) + 1))
                act.wait_ge(evacuated[NM - 1], M_BASE[c + 1] // NM + 1)
                for m in range(HT):
                    ins = act.activation(facc[:, m], facc[:, m], ACT.Silu, bias=col(C_B2, m))
                ins.then_inc(g_full, 1)

        @block.vector
        def _(dve):
            def quarter_drives(c, half, U, q):
                dve.tensor_tensor(work[:, q * Q:(q + 1) * Q, 1:], bbc[:, q * Q:(q + 1) * Q, :],
                                  dtu[:, :].unsqueeze(1).to_broadcast([P, Q, TS]), ALU.mult).then_inc(driven, 1)

            def quarter_scan(U, q):
                dve.wait_ge(driven, U * 4 + (q + 1))
                dve.wait_ge(decay_full, U * 4 + (q + 1))
                flat = work[:, q * Q:(q + 1) * Q, :].rearrange("p n t -> p (n t)")
                dve.tensor_tensor_scan(flat, decay[:, q % 2].rearrange("p n t -> p (n t)"), flat, 0.0,
                                       ALU.mult, ALU.add).then_inc(decay_free, 1)

            def scan_first(c, half, g, s, k, before=None):
                U = unit_no(c, half, g, s, k)
                dve.wait_ge(unit_in[k], 16 * (turn2(c, g, s, STEPS, 8 * half) + 1))
                dve.tensor_tensor(dtu[:, :], unit[:, k, 0], unit[:, k, 1], ALU.mult).then_inc(dtu_full, 1)
                if before:
                    skip(c, half, g, *before)
                if c % CPB == 0 and half == 0:
                    dve.memset(work[:, :, 0:1], 0.0)
                else:
                    dve.tensor_scalar(work[:, :, 0:1], carry[:, chan(g, s, k)].unsqueeze(2), 1.0, None, ALU.mult)
                dve.wait_ge(b_full, 16 * (2 * c + half + 1))
                dve.wait_ge(dtu_full, U + 1)
                quarter_drives(c, half, U, 0)
                if before:
                    gate(c, half, g, *before)
                quarter_drives(c, half, U, 1)
                quarter_scan(U, 0)
                quarter_drives(c, half, U, 2)
                quarter_scan(U, 1)

            def scan_rest(c, half, g, s, k):
                U = unit_no(c, half, g, s, k)
                quarter_drives(c, half, U, 3)
                quarter_scan(U, 2)
                quarter_scan(U, 3)
                dve.wait_ge(c_full, 16 * (2 * c + half + 1))
                dve.wait_ge(decay_free, U * 4 + 4)
                dve.tensor_tensor(work[:, 0:N // 2, 0:TS], work[:, 0:N // 2, 1:], cbc[:, 0:N // 2, :], ALU.mult)
                dve.wait_ge(decay_free, U * 4 + 6)
                dve.tensor_tensor(work[:, N // 2:, 0:TS], work[:, N // 2:, 1:], cbc[:, N // 2:, :], ALU.mult)\
                    .then_inc(weighted, 1)
                dve.tensor_scalar(carry[:, chan(g, s, k)].unsqueeze(2), work[:, :, TS:], 1.0, None, ALU.mult)\
                    .then_inc(carried, 1)
                dve.wait_ge(weighted, U + 1)
                dve.wait_ge(y_stored[k], 16 * (turn2(c, g, s, STEPS, 8 * half) + 1))
                dve.tensor_reduce(yt[:, k], work[:, :, 0:TS].rearrange("p n t -> p t n"), AX.X, ALU.add)\
                    .then_inc(summed, 1)

            def skip(c, half, g, s, k):
                dve.wait_ge(summed, unit_no(c, half, g, s, k) + 1)
                dve.scalar_tensor_tensor(out=yt[:, k], in0=unit[:, k, 1], scalar=par[:, bass.ds(chan(g, s, k) + C_D, 1)],
                                         in1=yt[:, k], op0=ALU.mult, op1=ALU.add).then_inc(skipped, 1)

            def gate(c, half, g, s, k):
                dve.wait_ge(skipped, unit_no(c, half, g, s, k) + 1)
                dve.tensor_tensor(yt[:, k], yt[:, k], unit[:, k, 2], ALU.mult).then_inc(unit_done, 1)

            def convolution(e, g, s, mring, *moffs):
                pair = g * S4 + (e * 8 + s)
                for j in range(K):
                    for k in range(2):
                        ch = chan(g, s, k)
                        w = par[:, bass.ds(ch * K + (C_CONVW + j), 1)]
                        if j == 0:
                            dve.wait_ge(evacuated[mring.slot(moffs[k])], mring.turn(g, moffs[k]) + 2)
                            dve.wait_ge(ut_stored[k], 16 * (turn2(e, g, s, 16) + 1))
                            dve.wait_ge(wssm_used, ch + (e * DT + 1))
                            ins = dve.tensor_scalar(ut[:, k], xin[:, k, 0:TC], w, None, ALU.mult)
                        else:
                            dve.wait_ge(conv_tap, pair * 6 + (2 * (j - 1) + k + 1))
                            ins = dve.scalar_tensor_tensor(out=ut[:, k], in0=xin[:, k, j:j + TC], scalar=w,
                                                           in1=ut[:, k], op0=ALU.mult, op1=ALU.add)
                        ins.then_inc(conv_tap if j < K - 1 else conv_done, 1)

            def output_add(c, half, g, s, k):
                wring, mring = w_ring(c, half), m_ring(c, half)
                b = mring.slot(m_off(c, s, "ffn", k))
                m = 4 * (s - 2) + k
                dve.wait_ge(product_done, wring.number(g, w_off(c, half, s, "ffn", k)) + W_DONE)
                dve.wait_ge(facc_zero, c + 1)
                dve.tensor_tensor(facc[:, m], pm[b][:, :], facc[:, m], ALU.add).then_inc(evacuated[b], 1)

            def combine(ring, off, e, g, s, base):
                idx = g * 2 + (HT * e + base + s // 2)
                dve.wait_ge(product_done, ring.number(g, off) + W_DONE)
                dve.wait_ge(gx_in, idx * 32 + 32)
                dve.tensor_tensor(gx[:, 0], p_out[:, :], gx[:, 0], ALU.mult).then_inc(d_free, 1)
                dve.wait_ge(d_free, idx + 2)
                dve.tensor_tensor(gx[:, 0], gx[:, 0], gx[:, 1], ALU.add).then_inc(out_ready, 1)

            def pre_dt_tiles(g, s):
                z, r, p, w = pre_dt(s)

                def chain(i):
                    dve.wait_ge(pre_chain, g * 24 + (6 * s + i))
                dve.wait_ge(pre_stored[s % 2], g * 64 + (32 * (s // 2) + 16))
                for k in range(2):
                    ch = chan(g, s, k)
                    dve.wait_ge(dt_full, ch + 1)
                    dve.tensor_scalar(z[:, k], p_st[k][:, :], par[:, bass.ds(ch + C_BDT, 1)], None, ALU.add)\
                        .then_inc(dt_bank_free, 1)
                dve.wait_ge(dt_bank_free, chan(g, s, 1) + DONE)
                dve.tensor_scalar(r, z, 0.0, None, ALU.max).then_inc(pre_chain, 1)
                chain(1)
                dve.scalar_tensor_tensor(out=z, in0=r, scalar=-2.0, in1=z, op0=ALU.mult, op1=ALU.add).then_inc(pre_chain, 1)
                dve.wait_ge(pre_exp, g * S4 + (s + 1))
                dve.tensor_scalar(w, p, 1.0, None, ALU.add).then_inc(pre_chain, 1)
                chain(3)
                dve.scalar_tensor_tensor(out=p, in0=w, scalar=-1.0, in1=p, op0=ALU.add, op1=ALU.subtract).then_inc(pre_chain, 1)
                dve.wait_ge(pre_ln, g * S4 + (s + 1))
                chain(4)
                dve.tensor_tensor(z, z, p, ALU.subtract).then_inc(pre_chain, 1)
                chain(5)
                dve.tensor_tensor(z, z, r, ALU.add).then_inc(pre_chain, 1)

            def dt_tile(e, g, s, k):
                n = chan(g, s, k) + (e - 1) * DT
                dve.wait_ge(dt_chain, n * 3 + 3)
                dve.scalar_tensor_tensor(out=dtb[:, 1], in0=dtb[:, 2], scalar=-1.0, in1=dtb[:, 1], op0=ALU.add,
                                         op1=ALU.subtract).then_inc(dt_sum, 1)
                dve.wait_ge(dt_sum, n * 3 + 4)
                dve.tensor_tensor(dtb[:, 3], dtb[:, 3], dtb[:, 1], ALU.subtract).then_inc(dt_sum, 1)
                dve.wait_ge(dt_sum, n * 3 + 5)
                dve.wait_ge(dt_stored, n * 16 + 16)
                dve.tensor_tensor(dtb[:, 4], dtb[:, 3], dtb[:, 0], ALU.add).then_inc(dt_sum, 1)

            def center(e):
                dve.wait_ge(mean_full, e + 1)
                for k in range(HT):
                    dve.tensor_tensor(xn[e % 2][:, k], xn[e % 2][:, k], p_st[0][:, :], ALU.subtract).then_inc(centered, 1)

            def normalise(e):
                x = xn[e % 2][:, :, :]
                dve.wait_ge(std_full, e + 1)
                dve.reciprocal(dtb[:, 2], dtb[:, 2]).then_inc(rstd_full, 1)
                dve.wait_ge(rstd_full, e + 1)
                dve.tensor_tensor(x, x, dtb[:, 2].unsqueeze(1).to_broadcast([P, HT, TC]), ALU.mult)\
                    .then_inc(xn_ready, 1)

            def ssm_norm(e):
                dve.wait_ge(srs_full, e + 1)
                dve.reciprocal(dtb[0:SROWS, 3], dtb[0:SROWS, 3]).then_inc(srs_inv, 1)
                dve.wait_ge(srs_inv, e + 1)
                dve.tensor_tensor(ssm[:, :], ssm[:, :], dtb[0:SROWS, 3], ALU.mult).then_inc(ssm_ready, 1)

            dve.sem_inc(product_done, NW)
            dve.sem_inc(dt_sum, 3)
            for free in (*evacuated, d_free):
                dve.sem_inc(free, 1)
            for free in (conv_done, wssm_used, dt_bank_free, unit_done, last_free):
                dve.sem_inc(free, 2)
            dve.memset(zeros[:, :], 0.0).then_inc(zeros_set, 1)
            for k in range(2):
                dve.memset(decay[:, k, :, 0:1], 0.0).then_inc(decay_free, 1)
            dve.wait_ge(aneg_exp, 1)
            dve.tensor_scalar(aneg[:, :], aneg[:, :], -1.0, None, ALU.mult).then_inc(aneg_full, 1)
            center(0)
            normalise(0)
            center(1)
            ring = pre_ring(0)
            with dve.Fori(0, 2) as g:
                for s in range(S4):
                    convolution(0, g, s, ring, 2 * s, 2 * s + 1)
            ssm_norm(0)
            normalise(1)
            with dve.Fori(0, 2) as g:
                for s in range(S4):
                    pre_dt_tiles(g, s)

            for c in range(NCH):
                more = c < NCH - 1
                for half in range(2):
                    with dve.Fori(0, 2) as g:
                        for s in range(S4):
                            scan_first(c, half, g, s, 0, (s - 1, 1) if s > 0 else None)
                            if more and half == 1 and s == 1:
                                dt_tile(c + 1, g, 0, 1)
                            scan_rest(c, half, g, s, 0)
                            if more and half == 1 and s > 0:
                                dt_tile(c + 1, g, s, 0)
                            if s >= 2:
                                output_add(c, half, g, s, 0)
                            scan_first(c, half, g, s, 1, (s, 0))
                            if more and half == 0:
                                convolution(c + 1, g, s, m_ring(c, half), m_off(c, s, "in", 0), m_off(c, s, "in", 1))
                            if s >= 2:
                                output_add(c, half, g, s, 1)
                            scan_rest(c, half, g, s, 1)
                            if s == S4 - 1:
                                skip(c, half, g, s, 1)
                                gate(c, half, g, s, 1)
                            if more and half == 1:
                                dt_tile(c + 1, g, s, 0 if s == 0 else 1)
                            if s >= 2:
                                output_add(c, half, g, s, 2)
                                output_add(c, half, g, s, 3)
                            if c > 0 and s % 2:
                                combine(w_ring(c, half), w_off(c, half, s, "out"), c - 1, g, s, 4 * half)
                    if more and half == 0:
                        ssm_norm(c + 1)
                if c + 2 < NCH:
                    center(c + 2)
                    normalise(c + 2)
            dve.wait_ge(g_full, NCH)
            dve.wait_ge(resid_in, 16)
            dve.wait_ge(last_free, HT + 2)
            dve.tensor_tensor(early, early, facc[:, :, 0:TS], ALU.mult).then_inc(early_full, 1)
            dve.wait_ge(early_full, 1)
            dve.tensor_tensor(early, early, resid[:, :, 0:TS], ALU.add).then_inc(early_ready, 1)
            for m in range(HT):
                dve.wait_ge(product_done, last_ring.number(0, HT + m) + W_DONE)
                dve.tensor_tensor(facc[:, m, TS:], p_last[m][:, 0:TS], facc[:, m, TS:], ALU.mult).then_inc(last_scaled, 1)
                dve.wait_ge(last_scaled, m + 1)
                dve.tensor_tensor(facc[:, m, TS:], facc[:, m, TS:], resid[:, m, TS:], ALU.add).then_inc(last_ready, 1)

        @block.gpsimd
        def _(pool):
            def store_input(e, half, g, s):
                for k in range(2):
                    ch = chan(g, s, k)
                    wait(pool, u_full if half == 0 else gate_full, ch + (e * DT + 1))
                    pool.dma_start(spill[ch, :, 1 + half, toks(e)], ut[:, k]).then_inc(ut_stored[k], 16)

            def store_dt(e, g, s, k):
                ch = chan(g, s, k)
                n = ch + (e - 1) * DT
                wait(pool, dt_sum, n * 3 + 6)
                pool.dma_start(spill[ch, :, 0, toks(e)], dtb[:, 4]).then_inc(dt_stored, 16)

            def store_bc(e):
                wait(pool, ssm_ready, e + 1)
                pool.dma_start(bc_d[:, toks(e)], ssm[R:SROWS, :]).then_inc(bc_stored, 16)

            def store_y(c, half, g, s, k):
                t0 = c * TC + half * TS
                wait(pool, unit_done, unit_no(c, half, g, s, k) + DONE)
                pool.dma_start(y_d[chan(g, s, k), :, t0:t0 + TS], yt[:, k]).then_inc(y_stored[k], 16)

            def load_gx(e, g, s, base):
                m = g * 2 + (base + s // 2)
                wait(pool, out_stored, (m + (HT * e + 1)) * 16)
                pool.dma_start(gx[:, 0], g_d[m, :, toks(e)]).then_inc(gx_in, 16)
                pool.dma_start(gx[:, 1], xT[m, :, toks(e)]).then_inc(gx_in, 16)

            def store_out(e, g, s, base):
                m = g * 2 + (base + s // 2)
                wait(pool, out_ready, m + (HT * e + 1))
                pool.dma_start(outT[m, :, toks(e)], gx[:, 0]).then_inc(out_stored, 16)

            def load_y(c):
                for k in range(2):
                    wait(pool, y_stored[k], 16 * (STEPS * (c + 1) + 1))
                if c > 0:
                    wait(pool, product_done, w_ring(c, 1).number(1, w_off(c, 1, 3, "out")) + W_DONE)
                pool.dma_start(yin[:, :, :], y_d[:, :, toks(c)].rearrange("k p t -> p k t")).then_inc(y_in, 16)

            def load_y_early():
                c = NCH - 1
                for k in range(2):
                    wait(pool, y_stored[k], 16 * (STEPS * c + 8 + 1))
                wait(pool, product_done, w_ring(c - 1, 1).number(1, w_off(c - 1, 1, 1, "ffn", 3)) + W_DONE)
                pool.dma_start(y_early, y_d[:, :, T - TC:T - TS].rearrange("k p t -> p k t")).then_inc(y_early_in, 16)

            for buf, stored in ((ut[:, 0], ut_stored[0]), (ut[:, 1], ut_stored[1]), (dtb[:, 4], dt_stored),
                                (yin[:, 0], pre_stored[0]), (yin[:, 8], pre_stored[1]),
                                (yt[:, 0], y_stored[0]), (yt[:, 1], y_stored[1]), (gx[:, 0], out_stored)):
                pool.dma_start(buf[:, 0:2], params[:, 0:2]).then_inc(stored, 16)
            pool.memset(facc[:, :, :], 0.0).then_inc(facc_zero, 1)
            for half in range(2):
                with pool.Fori(0, 2) as g:
                    for s in range(S4):
                        store_input(0, half, g, s)
                        if half == 1:
                            wait(pool, pre_chain, g * 24 + (6 * s + 6))
                            for k in range(2):
                                pool.dma_start(spill[chan(g, s, k), :, 0, toks(0)], pre_dt(s)[0][:, k]).then_inc(pre_stored[s % 2], 16)
                if half == 0:
                    store_bc(0)

            for c in range(NCH):
                more = c < NCH - 1
                for half in range(2):
                    with pool.Fori(0, 2) as g:
                        for s in range(S4):
                            if c > 0 and s % 2 == 0:
                                load_gx(c - 1, g, s, 4 * half)
                            if more and half == 1 and s == 1:
                                store_dt(c + 1, g, 0, 1)
                            if more and half == 1 and s > 0:
                                store_dt(c + 1, g, s, 0)
                            store_y(c, half, g, s, 0)
                            if more:
                                store_input(c + 1, half, g, s)
                            if more and half == 1:
                                store_dt(c + 1, g, s, 0 if s == 0 else 1)
                            store_y(c, half, g, s, 1)
                            if c > 0 and s % 2:
                                store_out(c - 1, g, s, 4 * half)
                    if half == 0:
                        if more:
                            store_bc(c + 1)
                        else:
                            load_y_early()
                if more:
                    load_y(c)
                    wait(pool, g_full, c + 1)
                    pool.dma_start(g_d[:, :, toks(c)].rearrange("m p t -> p m t"), facc[:, :, :]).then_inc(g_stored, 16)
                    wait(pool, g_stored, 16 * (c + 1))
                    pool.memset(facc[:, :, :], 0.0).then_inc(facc_zero, 1)
            wait(pool, out_stored, 16 * (HT * (NCH - 1) + 1))


def kernel(**inputs):
    import numpy as np
    import concourse.bacc as bacc
    from concourse.bass_utils import run_bass_kernel_spmd

    def arr(name):
        return np.asarray(inputs[name])

    def tiles(w):
        k, m = w.shape
        w = w.reshape(k // H, 8, P, m // P, P).transpose(3, 0, 2, 1, 4)
        return np.ascontiguousarray(w).reshape(m // P, k // H, P, 8 * P)

    def channels(v, n):
        return v.reshape(-1, P, n).transpose(1, 0, 2).reshape(P, -1)

    x = arr("L0_attn_hidden_states")
    w_in = arr("L0_attn_W_in").T
    blk = np.zeros((P, SROWS), np.float32)
    for a, n in ((0, R), (R, N), (R + N, N)):
        blk[a:a + n, a:a + n] = 1.0 / n
    consts = np.zeros((P, NPAR - C_ONES), np.float32)
    consts[:, 0:P] = 1.0 / H
    consts[:, C_BLK - C_ONES:C_BLK - C_ONES + SROWS] = blk
    consts[:, C_EPS - C_ONES] = LN_EPS
    consts[:, C_EPS - C_ONES + 1] = RMS_EPS
    params = np.concatenate([
        channels(arr("L0_attn_conv_w"), K), channels(arr("L0_attn_conv_b"), 1), channels(arr("L0_attn_b_dt"), 1),
        channels(arr("L0_attn_D"), 1), channels(arr("L0_attn_A_log"), N), channels(arr("L0_ffn_inter_b"), 1),
        channels(arr("L0_ffn_output_b"), 1), consts], axis=1)
    arrays = {
        "xT": np.ascontiguousarray(x.reshape(T, H).T).reshape(HT, P, T),
        "params": np.ascontiguousarray(params),
        "w_x": tiles(w_in[:, :D_IN])[:, 0],
        "w_g": tiles(w_in[:, D_IN:])[:, 0],
        "w_1": tiles(arr("L0_ffn_inter_w"))[:, 0],
        "w_2": np.ascontiguousarray(tiles(arr("L0_ffn_output_w")).transpose(1, 0, 2, 3)).reshape(FT, P, 8 * P),
        "w_o": tiles(arr("L0_attn_W_out").T).reshape(DT, P, 8 * P),
        "w_ssm": np.ascontiguousarray(arr("L0_attn_W_x").T).reshape(DT, P, SROWS),
        "w_dt": np.ascontiguousarray(arr("L0_attn_W_dt").reshape(DT, P, R).transpose(0, 2, 1)),
    }
    nc = bacc.Bacc("TRN2", target_bir_lowering=False, num_devices=1)
    args = {}
    maps = {}
    for name, a in arrays.items():
        maps[f"in_{name}"] = np.ascontiguousarray(a)
        args[name] = nc.dram_tensor(f"in_{name}", a.shape, mybir.dt.from_np(a.dtype), kind="ExternalInput").ap()
    args["outT"] = nc.dram_tensor("out_0", (HT, P, T), F32, kind="ExternalOutput").ap()
    build(nc, **args)
    r = run_bass_kernel_spmd(nc, [maps], core_ids=[0])
    got = r.results[0]["out_0"]
    return np.ascontiguousarray(np.asarray(got).reshape(H, T).T).reshape(B, L, H)
```

```python
from contextlib import ExitStack

import concourse.bass as bass
from concourse import mybir

F32 = mybir.dt.float32
ALU = mybir.AluOpType
ACT = mybir.ActivationFunctionType
AX = mybir.AxisListType

P = 128
H = 1024
D_IN = 2048
N = 16
K = 4
R = 64
F = 4096
B, L = 2, 1024
T = B * L
LN_EPS, RMS_EPS = 1e-5, 1e-6

TC = 512
NCH = T // TC
CPB = L // TC
HT = H // P
DT = D_IN // P
FT = F // P
GRP = 8
STEPS = 16
S4 = 4
TS = 256
Q = 4
NQ = N // Q
SROWS = R + 2 * N
NW = 4
NM = 4

C_CONVW = 0
C_CONVB = C_CONVW + DT * K
C_BDT = C_CONVB + DT
C_D = C_BDT + DT
C_ALOG = C_D + DT
C_B1 = C_ALOG + DT * N
C_B2 = C_B1 + FT
C_ONES = C_B2 + HT
C_BLK = C_ONES + P
C_EPS = C_BLK + SROWS
NPAR = C_EPS + 2


def step_tiles(c, half, s, late=False):
    ins, ffn = [("in", k) for k in range(2)], [("ffn", k) for k in range(4)]
    if c == NCH - 1:
        kind = "early" if half == 1 else "rest"
        tiles = ffn[:2] + [(kind, 0), (kind, 1)] + ffn[2:]
    else:
        tiles = ffn[:2] + ins + ffn[2:] if s == 0 else ins + ffn
        if late:
            tiles = tiles[:4] + [("late", 0)] + tiles[4:] + [("late", 1)]
    return tiles + ([("out", 0)] if c > 0 else [])


def w_per_step(c, half):
    return len(step_tiles(c, half, 0))


def m_per_step(c):
    return 4 + (2 if c < NCH - 1 else 0)


LATE = DT // 2
PRE_TILES = 2 * DT - LATE
W_BASE = [PRE_TILES + (LATE if c > 0 else 0) + STEPS // 2 * sum(w_per_step(b, h) for b in range(c) for h in range(2))
          for c in range(NCH + 1)]
M_BASE = [PRE_TILES + STEPS * sum(m_per_step(b) for b in range(c)) for c in range(NCH + 1)]
assert all(b % NW == 0 for b in W_BASE) and all(b % NM == 0 for b in M_BASE)


class Ring:

    def __init__(self, base, per, n):
        self.base, self.per, self.n = base, per, n

    def slot(self, off):
        return off % self.n

    def turn(self, g, off):
        return g * (self.per * S4 // self.n) + (self.base // self.n + off // self.n)

    def number(self, g, off):
        return g * (self.per * S4) + (self.base + off)


def build(nc, xT, params, w_x, w_g, w_1, w_2, w_o, w_ssm, w_dt, outT):
    spill = nc.dram_tensor("spill", (DT, P, 3, T), F32, kind="Internal").ap()
    y_d = nc.dram_tensor("y_d", (DT, P, T), F32, kind="Internal").ap()
    g_d = nc.dram_tensor("g_d", (HT, P, T), F32, kind="Internal").ap()
    bc_d = nc.dram_tensor("bc_d", (2 * N, T), F32, kind="Internal").ap()

    ctx = ExitStack()
    with ctx:
        def sb(name, shape):
            return ctx.enter_context(nc.sbuf_tensor(name, shape, F32))

        def ps(name):
            return ctx.enter_context(nc.psum_tensor(name, [P, TC], F32))

        def sem(name):
            return ctx.enter_context(nc.semaphore(name))

        def sems(name, n):
            return [sem(f"{name}{i}") for i in range(n)]

        par = sb("par", [P, NPAR])
        xn = [sb(f"xn{i}", [P, HT, TC]) for i in range(2)]
        wts = sb("wts", [P, NW, 8, P])
        hid = sb("hid", [P, GRP, TC])
        facc = sb("facc", [P, HT, TC])
        yin = sb("yin", [P, DT, TC])
        bbc = sb("bbc", [P, N, TS])
        cbc = sb("cbc", [P, N, TS])
        work = sb("work", [P, N, TS + 1])
        decay = sb("decay", [P, 2, Q, TS + 1])
        unit = sb("unit", [P, 2, 3, TS])
        dtu = sb("dtu", [P, TS])
        yt = sb("yt", [P, 2, TS])
        xin = sb("xin", [P, 2, K - 1 + TC])
        ut = sb("ut", [P, 2, TC])
        dtb = sb("dtb", [P, 5, TC])
        ssm = sb("ssm", [SROWS, TC])
        gx = sb("gx", [P, 2, TC])
        wssm = sb("wssm", [P, 2, SROWS])
        wdt = sb("wdt", [R, 2, P])
        aneg = sb("aneg", [P, DT * N])
        carry = sb("carry", [P, DT, N])
        halo = sb("halo", [P, DT, K - 1])
        zeros = sb("zeros", [P, K])

        pm = [ps(f"pm{i}") for i in range(NM)]
        p_out, p_ssm = ps("p_out"), ps("p_ssm")
        p_st = [ps("p_st0"), ps("p_st1")]

        pre_wssm = hid[:, :, :].rearrange("p k t -> p (k t)")[:, 0:2 * S4 * SROWS].rearrange("p (n m) -> p n m", m=SROWS)
        y_rest = xn[NCH % 2][:, :, :].rearrange("p k t -> p (k t)").rearrange("p (d t) -> p d t", t=TS)
        t_rest = (NCH - 3) * TC + TS
        y_early = xn[NCH % 2][:, :, :].rearrange("p k t -> p (k t)").rearrange("p (d t) -> p d t", t=TS)
        early = dtb[:, 0:4].rearrange("p b t -> p (b t)").rearrange("p (m t) -> p m t", t=TS)
        resid = xn[(NCH - 1) % 2][:, :, :]
        p_last = [p_ssm, *pm[0:3], *p_st, pm[3], p_out]

        params_in, zeros_set, aneg_exp, aneg_full = sem("params_in"), sem("zeros_set"), sem("aneg_exp"), sem("aneg_full")
        w_full, product_done, evacuated = sems("w_full", NW), sem("product_done"), sems("evacuated", NM)
        x_in, mean_full, centered = sems("x_in", 2), sem("mean_full"), sem("centered")
        sq_full, sq_used, var_full, std_full = sem("sq_full"), sem("sq_used"), sem("var_full"), sem("std_full")
        rstd_full, xn_ready = sem("rstd_full"), sem("xn_ready")
        conv_tap, conv_done = sem("conv_tap"), sem("conv_done")
        u_full, gate_full, ut_stored = sem("u_full"), sem("gate_full"), sems("ut_stored", 2)
        wssm_full, wssm_used, wdt_full = sems("wssm_full", 2), sem("wssm_used"), sems("wdt_full", 2)
        ssm_full, ssm_evac, ssq_full, ms_full = sem("ssm_full"), sem("ssm_evac"), sem("ssq_full"), sem("ms_full")
        srs_full, srs_inv, ssm_ready, bc_stored = sem("srs_full"), sem("srs_inv"), sem("ssm_ready"), sem("bc_stored")
        dt_full, dt_bank_free, dt_chain = sem("dt_full"), sem("dt_bank_free"), sem("dt_chain")
        dt_sum, dt_stored = sem("dt_sum"), sem("dt_stored")
        b_full, c_full, unit_in = sem("b_full"), sem("c_full"), sems("unit_in", 2)
        decay_full, decay_free = sem("decay_full"), sem("decay_free")
        dtu_full, driven, carried, weighted = sem("dtu_full"), sem("driven"), sem("carried"), sem("weighted")
        summed, skipped, unit_done, y_stored = sem("summed"), sem("skipped"), sem("unit_done"), sems("y_stored", 2)
        h_full, facc_zero, g_full, g_stored = sem("h_full"), sem("facc_zero"), sem("g_full"), sem("g_stored")
        y_in, d_full, d_free = sem("y_in"), sem("d_full"), sem("d_free")
        gx_in, out_ready, out_stored = sem("gx_in"), sem("out_ready"), sem("out_stored")

        y_early_in, y_last_in, last_free, resid_in = sem("y_early_in"), sems("y_last_in", 2), sem("last_free"), sem("resid_in")
        early_full, early_ready, last_ready, last_stored = sem("early_full"), sem("early_ready"), sem("last_ready"), sem("last_stored")
        pre_wssm_full, pre_chain, pre_exp, pre_ln = sem("pre_wssm_full"), sem("pre_chain"), sem("pre_exp"), sem("pre_ln")
        pre_stored, late_full, late_stored = sems("pre_stored", 2), sem("late_full"), sems("late_stored", 2)
        last_scaled = sem("last_scaled")
        y_rest_in, rest_in, rest_ready, rest_stored = sem("y_rest_in"), sems("rest_in", 2), sem("rest_ready"), sems("rest_stored", 2)
        waits_met = sem("waits_met")

        DONE = 3
        W_DONE = NW + 1

        def col(base, i=0, n=1):
            return par[:, base + i:base + i + n]

        def toks(e):
            return slice(e * TC, (e + 1) * TC)

        def chan(g, s, k):
            return g * (2 * S4) + (2 * s + k)

        def unit_no(c, half, g, s, k):
            return g * (2 * S4) + (c * 2 * STEPS + half * STEPS + 2 * s + k)

        def turn2(e, g, s, per=8, base=0):
            return g * S4 + (e * per + base + s)

        def m_off(c, s, kind, k=0):
            return s * m_per_step(c) + [t for t in step_tiles(c, 0, s) if t[0] in ("in", "ffn")].index((kind, k))

        def w_off(c, half, g, s, kind, k=0):
            if c == 0 and half == 0:
                late = g == 0
                return g * S4 * (w_per_step(0, 0) + 2) + s * (w_per_step(0, 0) + 2 * late) \
                    + step_tiles(0, 0, s, late).index((kind, k))
            return s * w_per_step(c, half) + step_tiles(c, half, s).index((kind, k))

        def w_ring(c, half):
            if c == 0 and half == 0:
                return Ring(W_BASE[0], 0, NW)
            late = LATE if c == 0 else 0
            return Ring(W_BASE[c] + late + half * 8 * w_per_step(c, 0), w_per_step(c, half), NW)

        def steps_of(eng, c, half, steps):
            if c == 0 and half == 0:
                steps(0)
                steps(1)
            else:
                with eng.Fori(0, 2) as g:
                    steps(g)

        def late_in(c, half, g):
            return c == 0 and half == 0 and g == 0

        def late_before(c, half, g, s):
            if c == 0 and half == 0 and 0 < g * S4 + s <= S4:
                return g * S4 + s - 1

        def ut_turn(e, half, g, s):
            return g * S4 + (e * 2 * 8 + half * 8 + s - (LATE // 2 if e > 0 else 0))

        def out_tokens(e):
            return TS if e == NCH - 3 else TC

        def gate_count(e, g, s, k):
            return chan(g, s, k) + (e * DT + 1 - (LATE if e > 0 else 0))

        def m_ring(c, half):
            return Ring(M_BASE[c] + half * 8 * m_per_step(c), m_per_step(c), NM)

        def pre_ring(half):
            return Ring(half * DT, 2, NW)

        last_ring = Ring(W_BASE[NCH], 1, NW)

        def wait(eng, semaphore, count):
            eng.wait_ge(semaphore, count)
            if not isinstance(count, int):
                eng.sem_inc(waits_met, 1)

        def broadcast_b(eng, c, half):
            t0 = c * TC + half * TS
            eng.wait_ge(bc_stored, 16 * (c + 1))
            if c + half > 0:
                eng.wait_ge(driven, 4 * STEPS * (2 * c + half))
            eng.dma_start(bbc[:, :, :], bc_d[0:N, t0:t0 + TS].partition_broadcast(P)).then_inc(b_full, 16)

        def broadcast_c(eng, c, half):
            t0 = c * TC + half * TS
            if c + half > 0:
                eng.wait_ge(weighted, STEPS * (2 * c + half))
            eng.dma_start(cbc[:, :, :], bc_d[N:2 * N, t0:t0 + TS].partition_broadcast(P)).then_inc(c_full, 16)

        def pre_dt(s):
            return [yin[:, 8 * (s % 2) + 2 * i:8 * (s % 2) + 2 * i + 2] for i in range(4)]

        block = ctx.enter_context(nc.Block())

        @block.sync
        def _(sp):
            def weight(ring, g, off, src):
                slot = ring.slot(off)
                wait(sp, product_done, ring.number(g, off) + 1)
                sp.dma_start(wts[:, slot].rearrange("p k m -> p (k m)"), src).then_inc(w_full[slot], 16)

            def ssm_weights(e, g, s):
                for k in range(2):
                    wait(sp, wssm_used, chan(g, s, k) + (e * DT + 1))
                    sp.dma_start(wssm[:, k], w_ssm[chan(g, s, k)]).then_inc(wssm_full[k], 16)

            def dt_weights(e, g, s):
                for k in range(2):
                    wait(sp, dt_bank_free, chan(g, s, k) + (e * DT + 1))
                    sp.dma_start(wdt[:, k], w_dt[chan(g, s, k)]).then_inc(wdt_full[k], 16)

            def x_chunk(e):
                sp.dma_start(xn[e % 2][:, :, :], xT[:, :, toks(e)].rearrange("k p t -> p k t")).then_inc(x_in[e % 2], 16)

            def scan_unit(c, half, g, s, k):
                wait(sp, unit_done, unit_no(c, half, g, s, k) + 1)
                if half == 0:
                    if c == 0 and g == 1:
                        wait(sp, late_stored[k], 16 * (s + 2))
                    else:
                        wait(sp, ut_stored[k], 16 * (ut_turn(c, 1, g, s) + 2))
                    if c == 0:
                        wait(sp, pre_stored[s % 2], g * 64 + (16 + 32 * (s // 2 + 1)))
                    else:
                        wait(sp, dt_stored, 16 * (chan(g, s, k) + ((c - 1) * DT + 2)))
                t0 = c * TC + half * TS
                sp.dma_start(unit[:, k], spill[chan(g, s, k), :, :, t0:t0 + TS]).then_inc(unit_in[k], 16)

            def load_y_last(j):
                c = NCH - 1
                wait(sp, product_done, w_ring(c, 1).number(1, w_off(c, 1, 1, 2 + j, "out")) + W_DONE)
                for k in range(2):
                    wait(sp, y_stored[k], 16 * (STEPS * c + 8 + 4 * (j + 1) + 1))
                sp.dma_start(yin[:, 8 * j:8 * j + 8, 0:TS],
                             y_d[8 * j:8 * j + 8, :, T - TS:T].rearrange("k p t -> p k t")).then_inc(y_last_in[j], 16)

            sp.dma_start(par[:, :], params).then_inc(params_in, 16)
            x_chunk(0)
            x_chunk(1)
            sp.dma_start(pre_wssm, w_ssm[0:2 * S4].rearrange("n p m -> p n m")).then_inc(pre_wssm_full, 16)
            ring = pre_ring(0)
            for g in range(2):
                for s in range(S4):
                    for k in range(2):
                        weight(ring, g, 2 * s + k, w_x[chan(g, s, k)])
                    if g == 1 and s == 0:
                        sp.wait_ge(wssm_used, 2 * S4 + 2)
                        sp.dma_start(pre_wssm, w_ssm[2 * S4:].rearrange("n p m -> p n m")).then_inc(pre_wssm_full, 16)
            ring = pre_ring(1)
            for s in range(S4):
                for k in range(2):
                    weight(ring, 0, 2 * s + k, w_g[chan(0, s, k)])
                dt_weights(0, 0, s)
            broadcast_b(sp, 0, 0)
            broadcast_c(sp, 0, 0)

            for c in range(NCH):
                for half in range(2):
                    ring = w_ring(c, half)
                    def steps(g):
                        for s in range(S4):
                            for kind, k in step_tiles(c, half, s, late_in(c, half, g)):
                                src = {"late": (w_g, chan(1, s, k)),
                                       "in": (w_x if half == 0 else w_g, chan(g, s, k)),
                                       "ffn": (w_1 if s < 2 else w_2, g * GRP + (2 * half * GRP + 4 * (s % 2) + k)),
                                       "rest": (w_o, g * (2 * S4) + (2 * s + k)),
                                       "early": (w_o, g * (2 * S4) + (2 * s + k)),
                                       "out": (w_o, g * S4 + (2 * half * S4 + s))}[kind]
                                weight(ring, g, w_off(c, half, g, s, kind, k), src[0][src[1]])
                                if (kind, k) == ("ffn", 0):
                                    scan_unit(c, half, g, s, 0)
                                if (kind, k) == ("ffn", 3):
                                    scan_unit(c, half, g, s, 1)
                                if c < NCH - 1 and half == 0 and (kind, k) == ("ffn", 1):
                                    ssm_weights(c + 1, g, s)
                                if c < NCH - 1 and half == 1 and (kind, k) == ("ffn", 2 if s == 0 else 1):
                                    dt_weights(c + 1, g, s)
                                if (kind, k) == ("late", 1):
                                    dt_weights(0, 1, s)
                    steps_of(sp, c, half, steps)
                if c + 2 < NCH:
                    wait(sp, product_done, w_ring(c, 1).number(1, w_off(c, 1, 1, 1, "ffn", 3)) + W_DONE)
                    x_chunk(c + 2)
            load_y_last(0)
            wait(sp, product_done, w_ring(NCH - 1, 1).number(1, w_off(NCH - 1, 1, 1, 1, "ffn", 3)) + W_DONE)
            sp.dma_start(resid, xT[:, :, toks(NCH - 1)].rearrange("k p t -> p k t")).then_inc(resid_in, 16)
            for i in range(2 * HT):
                if i == 6:
                    load_y_last(1)
                weight(last_ring, 0, i, w_o[2 * (i % HT) + i // HT])
            sp.wait_ge(early_ready, 1)
            sp.dma_start(outT[:, :, T - TC:T - TS].rearrange("m p t -> p m t"), early).then_inc(last_stored, 16)
            for m in range(HT):
                sp.wait_ge(last_ready, m + 1)
                sp.dma_start(outT[m, :, T - TS:T], facc[:, m, TS:]).then_inc(last_stored, 16)
            sp.wait_ge(last_stored, 16 * (HT + 1))

        @block.tensor
        def _(pe):
            def product(out, ring, g, off, rhs, start=True, stop=True):
                slot = ring.slot(off)
                pe.wait_ge(w_full[slot], 16 * (ring.turn(g, off) + 1))
                for k in range(8):
                    mm = pe.matmul(out, lhsT=wts[:, slot, k], rhs=rhs[:, k],
                                   start=start and k == 0, stop=stop and k == 7)
                mm.then_inc(product_done, 1)

            def ring_product(wring, mring, g, woff, moff, rhs):
                b = mring.slot(moff)
                pe.wait_ge(evacuated[b], mring.turn(g, moff) + 1)
                product(pm[b][:, :], wring, g, woff, rhs)

            def out_product(wring, g, woff, e, s, base=0):
                if s % 2 == 0:
                    pe.wait_ge(y_in, 16 * (e + 1))
                    pe.wait_ge(d_free, g * 2 + (HT * e + base + s // 2 + 1))
                n = out_tokens(e)
                product(p_out[:, 0:n], wring, g, woff, yin[:, 8 * (s % 2):8 * (s % 2) + 8, 0:n],
                        start=s % 2 == 0, stop=s % 2 == 1)

            def last_product(wring, g, woff, s, j, rhs, n):
                if j == 0:
                    pe.wait_ge(last_free, n + 1)
                product(p_st[s % 2][:, 0:TS], wring, g, woff, rhs, start=j == 0, stop=j == 1)

            def mean_sum(e):
                pe.wait_ge(x_in[e % 2], 16 * (e // 2 + 1))
                if e > 0:
                    pe.wait_ge(centered, HT * e)
                for k in range(HT):
                    mm = pe.matmul(p_st[0][:, :], lhsT=col(C_ONES, 0, P), rhs=xn[e % 2][:, k],
                                   start=k == 0, stop=k == HT - 1)
                mm.then_inc(mean_full, 1)

            def square_sum(e):
                for k in range(HT):
                    pe.wait_ge(sq_full, HT * e + k + 1)
                    pe.matmul(p_st[1][:, :], lhsT=col(C_ONES, 0, P), rhs=dtb[:, k % 2],
                              start=k == 0, stop=k == HT - 1).then_inc(sq_used, 1)

            def ssm_open(e):
                if e == 0:
                    pe.wait_ge(zeros_set, 1)
                if e > 0:
                    pe.wait_ge(srs_full, e)
                pe.matmul(p_ssm[0:SROWS, :], lhsT=col(C_BLK, 0, SROWS), rhs=zeros[:, 0:1].to_broadcast([P, TC]),
                          start=True, stop=False, skip_group_check=True)

            def ssm_close(e):
                pe.matmul(p_ssm[0:SROWS, :], lhsT=col(C_BLK, 0, SROWS), rhs=zeros[:, 0:1].to_broadcast([P, TC]),
                          start=False, stop=True, skip_group_check=True).then_inc(ssm_full, 1)

            def ssm_products(e, g, s):
                for k in range(2):
                    if e == 0:
                        pe.wait_ge(pre_wssm_full, g * 16 + 16)
                    else:
                        pe.wait_ge(wssm_full[k], 16 * (turn2(e - 1, g, s) + 1))
                    pe.wait_ge(u_full, chan(g, s, k) + (e * DT + 1))
                    pe.matmul(p_ssm[0:SROWS, :], lhsT=pre_wssm[:, 2 * s + k] if e == 0 else wssm[:, k], rhs=ut[:, k],
                              start=False, stop=False, skip_group_check=True).then_inc(wssm_used, 1)

            def ssm_square_means(e):
                pe.wait_ge(ssq_full, e + 1)
                pe.matmul(p_ssm[0:SROWS, :], lhsT=par[0:SROWS, C_BLK:C_BLK + SROWS],
                          rhs=dtb[0:SROWS, 3], start=True, stop=True).then_inc(ms_full, 1)

            def dt_product(e, g, s, k):
                n = chan(g, s, k) + e * DT
                pe.wait_ge(wdt_full[k], 16 * (turn2(e, g, s) + 1))
                pe.wait_ge(ssm_ready, e + 1)
                pe.wait_ge(dt_bank_free, n + 1)
                pe.matmul(p_st[k][:, :], lhsT=wdt[:, k], rhs=ssm[0:R, :], start=True, stop=True)\
                    .then_inc(dt_full, 1)

            pe.wait_ge(params_in, 16)
            mean_sum(0)
            square_sum(0)
            mean_sum(1)
            pe.wait_ge(xn_ready, 1)
            ssm_open(0)
            ring = pre_ring(0)
            with pe.Fori(0, 2) as g:
                for s in range(S4):
                    for k in range(2):
                        ring_product(ring, ring, g, 2 * s + k, 2 * s + k, xn[0])
                    if s > 0:
                        ssm_products(0, g, s - 1)
                ssm_products(0, g, S4 - 1)
            square_sum(1)
            ssm_close(0)
            ssm_square_means(0)
            ring = pre_ring(1)
            for s in range(S4):
                for k in range(2):
                    ring_product(ring, ring, 0, 2 * s + k, 2 * s + k, xn[0])
                dt_product(0, 0, s, 0)
                dt_product(0, 0, s, 1)

            for c in range(NCH):
                more = c < NCH - 1
                if more:
                    ssm_open(c + 1)
                for half in range(2):
                    if not more and half == 1:
                        pe.wait_ge(last_free, HT + 2)
                    wring, mring = w_ring(c, half), m_ring(c, half)
                    def steps(g):
                        for s in range(S4):
                            for kind, k in step_tiles(c, half, s, late_in(c, half, g)):
                                woff = w_off(c, half, g, s, kind, k)
                                if kind == "in":
                                    if s == 0:
                                        pe.wait_ge(xn_ready, c + 2)
                                    ring_product(wring, mring, g, woff, m_off(c, s, "in", k), xn[(c + 1) % 2])
                                elif kind == "ffn":
                                    if s == 2 and k == 0:
                                        pe.wait_ge(h_full, g * 2 + (c * 8 + half * 4 + 2))
                                    ring_product(wring, mring, g, woff, m_off(c, s, "ffn", k), xn[c % 2] if s < 2 else hid)
                                elif kind == "late":
                                    pe.wait_ge(late_full, 2 * s + k + 1)
                                    product(p_out[:, :], wring, g, woff, xn[0])
                                elif kind == "early":
                                    pe.wait_ge(y_early_in, 16)
                                    last_product(wring, g, woff, s, k, y_early[:, 8 * k:8 * k + 8], g * S4 + (HT + s))
                                elif kind == "rest":
                                    if k == 0:
                                        pe.wait_ge(dt_bank_free, 2 + DT * NCH)
                                        pe.wait_ge(y_rest_in, 16)
                                    last_product(wring, g, woff, s, k, y_rest[:, 8 * k:8 * k + 8], g * S4 + s)
                                else:
                                    if more and half == 0:
                                        ssm_products(c + 1, g, s)
                                    out_product(wring, g, woff, c - 1, s, 4 * half)
                                if more and half == 1 and (kind, k) == ("in", 1):
                                    dt_product(c + 1, g, s, 0)
                                if more and half == 1 and (kind, k) == ("ffn", 2 if s == 0 else 1):
                                    dt_product(c + 1, g, s, 1)
                            if c == 0 and half == 0:
                                ssm_products(c + 1, g, s)
                            if late_in(c, half, g):
                                dt_product(0, 1, s, 0)
                                dt_product(0, 1, s, 1)
                    steps_of(pe, c, half, steps)
                    if c < NCH - 1 and half == 0:
                        ssm_close(c + 1)
                        ssm_square_means(c + 1)
                if c + 2 < NCH:
                    pe.wait_ge(dt_bank_free, 2 + DT * (c + 2))
                    mean_sum(c + 2)
                    square_sum(c + 2)
            for i in range(2 * HT):
                j, m = i // HT, i % HT
                if i == 0:
                    for bank in evacuated:
                        pe.wait_ge(bank, M_BASE[NCH] // NM + 1)
                if i == 4:
                    pe.wait_ge(last_free, 2 * HT + 2)
                if i == HT - 1:
                    pe.wait_ge(d_free, HT * (NCH - 1) + 1)
                if m == 0:
                    pe.wait_ge(y_last_in[j], 16)
                product(p_last[m][:, 0:TS], last_ring, 0, i, yin[:, 8 * j:8 * j + 8, 0:TS], start=j == 0, stop=j == 1)

        @block.scalar
        def _(act):
            def decays(c, half, g, s, k, quarters):
                U = unit_no(c, half, g, s, k)
                if quarters[0] == 0:
                    act.wait_ge(unit_in[k], 16 * (turn2(c, g, s, STEPS, 8 * half) + 1))
                for q in quarters:
                    act.wait_ge(decay_free, U * 4 + (q + 1))
                    for i in range(Q):
                        a = chan(g, s, k) * N + (q * Q + i)
                        ins = act.activation(decay[:, q % 2, i, 1:], unit[:, k, 0], ACT.Exp, scale=aneg[:, bass.ds(a, 1)])
                    ins.then_inc(decay_full, 1)

            def input_tile(e, half, g, s, k, wring, woff, mring, moff):
                b = mring.slot(moff)
                ch = chan(g, s, k)
                act.wait_ge(product_done, wring.number(g, woff) + W_DONE)
                if half == 0:
                    act.wait_ge(conv_done, ch + (e * DT + 1))
                    first = e % CPB == 0
                    act.activation(xin[:, k, 0:K - 1], zeros[:, 0:K - 1] if first else halo[:, ch], ACT.Copy)
                    if first:
                        act.activation(halo[:, ch], pm[b][:, TC - K + 1:TC], ACT.Copy)
                    act.activation(xin[:, k, K - 1:], pm[b][:, :], ACT.Copy).then_inc(evacuated[b], 1)
                else:
                    act.wait_ge(ut_stored[k], 16 * (ut_turn(e, 1, g, s) + 1))
                    act.activation(ut[:, k], pm[b][:, :], ACT.Copy).then_inc(evacuated[b], 1)

            def input_silu(e, half, g, s, mring, *moffs):
                for k in range(2):
                    ch = chan(g, s, k)
                    if half == 0:
                        act.wait_ge(conv_done, ch + (e * DT + DONE))
                        act.activation(ut[:, k], ut[:, k], ACT.Silu, bias=par[:, bass.ds(ch + C_CONVB, 1)])\
                            .then_inc(u_full, 1)
                    else:
                        act.wait_ge(evacuated[mring.slot(moffs[k])], mring.turn(g, moffs[k]) + 2)
                        act.activation(ut[:, k], ut[:, k], ACT.Silu).then_inc(gate_full, 1)

            def hidden_tile(c, half, g, s, k):
                wring, mring = w_ring(c, half), m_ring(c, half)
                b = mring.slot(m_off(c, s, "ffn", k))
                act.wait_ge(product_done, wring.number(g, w_off(c, half, g, s, "ffn", k)) + W_DONE)
                act.activation(hid[:, 4 * s + k], pm[b][:, :], ACT.Identity,
                               bias=par[:, bass.ds(g * GRP + (C_B1 + 2 * half * GRP + 4 * s + k), 1)])\
                    .then_inc(evacuated[b], 1)

            def hidden_gelu(c, half, g, s):
                hidden_tile(c, half, g, s, 2)
                hidden_tile(c, half, g, s, 3)
                mring, moff = m_ring(c, half), m_off(c, s, "ffn", 3)
                act.wait_ge(evacuated[mring.slot(moff)], mring.turn(g, moff) + 2)
                act.activation(hid[:, 4 * s:4 * s + 4], hid[:, 4 * s:4 * s + 4], ACT.Gelu_apprx_tanh)\
                    .then_inc(h_full, 1)

            def dt_tile(e, g, s, k):
                ch = chan(g, s, k)
                n = ch + (e - 1) * DT
                bias = par[:, bass.ds(ch + C_BDT, 1)]
                act.wait_ge(xn_ready, 2)
                act.wait_ge(dt_full, n + (DT + 1))
                act.wait_ge(dt_sum, n * 3 + 3)
                act.activation(dtb[:, 0], p_st[k][:, :], ACT.Relu, bias=bias)
                act.activation(dtb[:, 1], p_st[k][:, :], ACT.Abs, bias=bias).then_inc(dt_bank_free, 1)
                act.wait_ge(dt_bank_free, n + (DT + DONE))
                act.activation(dtb[:, 1], dtb[:, 1], ACT.Exp, scale=-1.0).then_inc(dt_chain, 1)
                act.wait_ge(dt_chain, n * 3 + 1)
                act.activation(dtb[:, 2], dtb[:, 1], ACT.Identity, bias=1.0).then_inc(dt_chain, 1)
                act.wait_ge(dt_chain, n * 3 + 2)
                act.activation(dtb[:, 3], dtb[:, 2], ACT.Ln).then_inc(dt_chain, 1)

            def pre_dt_exp(g, s):
                minus_abs, _, p, w = pre_dt(s)
                act.wait_ge(pre_chain, g * 24 + (6 * s + 2))
                act.activation(p, minus_abs, ACT.Exp).then_inc(pre_exp, 1)

            def pre_dt_ln(g, s):
                z, _, p, w = pre_dt(s)
                act.wait_ge(pre_chain, g * 24 + (6 * s + 3))
                act.activation(z, w, ACT.Ln).then_inc(pre_ln, 1)

            def late_gate(s, k):
                act.wait_ge(product_done, w_ring(0, 0).number(0, w_off(0, 0, 0, s, "late", k)) + W_DONE)
                act.wait_ge(late_stored[k], 16 * (s + 1))
                act.activation(gx[:, k], p_out[:, :], ACT.Silu).then_inc(late_full, 1)

            def ssm_squares(e):
                act.wait_ge(ssm_full, e + 1)
                if e > 0:
                    act.wait_ge(bc_stored, 16 * e)
                if e > 1:
                    act.wait_ge(dt_sum, 3 * (DT * (e - 1) + 1))
                act.activation(ssm[:, :], p_ssm[0:SROWS, :], ACT.Copy).then_inc(ssm_evac, 1)
                act.wait_ge(ssm_evac, e + 1)
                act.activation(dtb[0:SROWS, 3], ssm[:, :], ACT.Square).then_inc(ssq_full, 1)

            def ssm_root(e):
                act.wait_ge(ms_full, e + 1)
                act.activation(dtb[0:SROWS, 3], p_ssm[0:SROWS, :], ACT.Sqrt, bias=par[0:SROWS, C_EPS + 1:C_EPS + 2])\
                    .then_inc(srs_full, 1)
                act.wait_ge(ssm_ready, e + 1)

            def layernorm(e):
                if e >= 2:
                    act.wait_ge(dt_sum, 3 * (DT * (e - 1) + 1))
                for k in range(HT):
                    if k >= 2:
                        act.wait_ge(sq_used, HT * e + k - 1)
                    act.wait_ge(centered, HT * e + k + 1)
                    act.activation(dtb[:, k % 2], xn[e % 2][:, k], ACT.Square).then_inc(sq_full, 1)
                act.wait_ge(sq_used, HT * (e + 1))
                act.activation(dtb[:, 2], p_st[1][:, :], ACT.Sqrt, bias=col(C_EPS)).then_inc(std_full, 1)

            def early_tile(g, s):
                c, half = NCH - 1, 1
                act.wait_ge(product_done, w_ring(c, half).number(g, w_off(c, half, g, s, "early", 1)) + W_DONE)
                act.activation(early[:, bass.ds(g * S4 + s, 1)], p_st[s % 2][:, 0:TS].unsqueeze(1), ACT.Copy)\
                    .then_inc(last_free, 1)

            act.wait_ge(params_in, 16)
            act.activation(aneg[:, :], col(C_ALOG, 0, DT * N), ACT.Exp).then_inc(aneg_exp, 1)
            layernorm(0)
            act.wait_ge(zeros_set, 1)
            ring = pre_ring(0)
            with act.Fori(0, 2) as g:
                for s in range(S4):
                    for k in range(2):
                        input_tile(0, 0, g, s, k, ring, 2 * s + k, ring, 2 * s + k)
                    input_silu(0, 0, g, s, ring, 2 * s, 2 * s + 1)
            layernorm(1)
            ssm_squares(0)
            ssm_root(0)
            ring = pre_ring(1)
            for s in range(S4):
                for k in range(2):
                    input_tile(0, 1, 0, s, k, ring, 2 * s + k, ring, 2 * s + k)
                input_silu(0, 1, 0, s, ring, 2 * s, 2 * s + 1)
                pre_dt_exp(0, s)
                pre_dt_ln(0, s)
            act.wait_ge(out_stored, 16)
            act.wait_ge(aneg_full, 1)

            for c in range(NCH):
                more = c < NCH - 1
                for half in range(2):
                    wring, mring = w_ring(c, half), m_ring(c, half)
                    if not more and half == 1:
                        for stored in rest_stored:
                            act.wait_ge(stored, 16 * (S4 + 1))
                    def steps(g):
                        for s in range(S4):
                            def input_of_next(k):
                                input_tile(c + 1, half, g, s, k, wring, w_off(c, half, g, s, "in", k),
                                           mring, m_off(c, s, "in", k))

                            before = late_before(c, half, g, s)
                            decays(c, half, g, s, 0, (0, 1))
                            if s in (1, 2):
                                hidden_gelu(c, half, g, s - 1)
                            if before is not None:
                                late_gate(before, 1)
                            decays(c, half, g, s, 0, (2, 3))
                            if s == 0:
                                hidden_tile(c, half, g, s, 0)
                                hidden_tile(c, half, g, s, 1)
                                decays(c, half, g, s, 1, (0, 1))
                                if more:
                                    input_of_next(0)
                                if before is not None:
                                    pre_dt_exp(1, before)
                                decays(c, half, g, s, 1, (2, 3))
                                if more:
                                    input_of_next(1)
                                    input_silu(c + 1, half, g, s, mring, m_off(c, s, "in", 0), m_off(c, s, "in", 1))
                                    if half == 1:
                                        dt_tile(c + 1, g, s, 0)
                            else:
                                if more:
                                    input_of_next(0)
                                    input_of_next(1)
                                    if half == 1:
                                        dt_tile(c + 1, g, s, 0)
                                decays(c, half, g, s, 1, (0, 1))
                                if s == 1:
                                    hidden_tile(c, half, g, s, 0)
                                if before is not None:
                                    pre_dt_exp(1, before)
                                decays(c, half, g, s, 1, (2, 3))
                                if more:
                                    input_silu(c + 1, half, g, s, mring, m_off(c, s, "in", 0), m_off(c, s, "in", 1))
                                if s == 1:
                                    hidden_tile(c, half, g, s, 1)
                            if before is not None:
                                pre_dt_ln(1, before)
                            if late_in(c, half, g):
                                late_gate(s, 0)
                            if more and half == 1:
                                dt_tile(c + 1, g, s, 1)
                            if c == NCH - 1 and half == 1:
                                early_tile(g, s)
                    steps_of(act, c, half, steps)
                    if half == 0 or more:
                        broadcast_b(act, c + half, 1 - half)
                    if more and half == 0:
                        ssm_squares(c + 1)
                        ssm_root(c + 1)
                    if half == 0 or more:
                        broadcast_c(act, c + half, 1 - half)
                if c + 2 < NCH:
                    layernorm(c + 2)
                if c == NCH - 2:
                    act.wait_ge(dt_sum, 3 * (DT * (NCH - 1) + 1))
                act.wait_ge(evacuated[NM - 1], M_BASE[c + 1] // NM + 1)
                for m in range(HT):
                    ins = act.activation(facc[:, m], facc[:, m], ACT.Silu, bias=col(C_B2, m))
                ins.then_inc(g_full, 1)

        @block.vector
        def _(dve):
            def quarter_drives(c, half, U, q):
                dve.tensor_tensor(work[:, q * Q:(q + 1) * Q, 1:], bbc[:, q * Q:(q + 1) * Q, :],
                                  dtu[:, :].unsqueeze(1).to_broadcast([P, Q, TS]), ALU.mult).then_inc(driven, 1)

            def quarter_scan(U, q):
                dve.wait_ge(driven, U * 4 + (q + 1))
                dve.wait_ge(decay_full, U * 4 + (q + 1))
                flat = work[:, q * Q:(q + 1) * Q, :].rearrange("p n t -> p (n t)")
                dve.tensor_tensor_scan(flat, decay[:, q % 2].rearrange("p n t -> p (n t)"), flat, 0.0,
                                       ALU.mult, ALU.add).then_inc(decay_free, 1)

            def scan_first(c, half, g, s, k, before=None):
                U = unit_no(c, half, g, s, k)
                dve.wait_ge(unit_in[k], 16 * (turn2(c, g, s, STEPS, 8 * half) + 1))
                dve.tensor_tensor(dtu[:, :], unit[:, k, 0], unit[:, k, 1], ALU.mult).then_inc(dtu_full, 1)
                if before:
                    skip(c, half, g, *before)
                if c % CPB == 0 and half == 0:
                    dve.memset(work[:, :, 0:1], 0.0)
                else:
                    dve.tensor_scalar(work[:, :, 0:1], carry[:, chan(g, s, k)].unsqueeze(2), 1.0, None, ALU.mult)
                dve.wait_ge(b_full, 16 * (2 * c + half + 1))
                dve.wait_ge(dtu_full, U + 1)
                quarter_drives(c, half, U, 0)
                if before:
                    gate(c, half, g, *before)
                quarter_drives(c, half, U, 1)
                quarter_scan(U, 0)
                quarter_drives(c, half, U, 2)
                quarter_scan(U, 1)

            def scan_rest(c, half, g, s, k):
                U = unit_no(c, half, g, s, k)
                quarter_drives(c, half, U, 3)
                quarter_scan(U, 2)
                quarter_scan(U, 3)
                dve.wait_ge(c_full, 16 * (2 * c + half + 1))
                dve.wait_ge(decay_free, U * 4 + 4)
                dve.tensor_tensor(work[:, 0:N // 2, 0:TS], work[:, 0:N // 2, 1:], cbc[:, 0:N // 2, :], ALU.mult)
                dve.wait_ge(decay_free, U * 4 + 6)
                dve.tensor_tensor(work[:, N // 2:, 0:TS], work[:, N // 2:, 1:], cbc[:, N // 2:, :], ALU.mult)\
                    .then_inc(weighted, 1)
                dve.tensor_scalar(carry[:, chan(g, s, k)].unsqueeze(2), work[:, :, TS:], 1.0, None, ALU.mult)\
                    .then_inc(carried, 1)
                dve.wait_ge(weighted, U + 1)
                dve.wait_ge(y_stored[k], 16 * (turn2(c, g, s, STEPS, 8 * half) + 1))
                dve.tensor_reduce(yt[:, k], work[:, :, 0:TS].rearrange("p n t -> p t n"), AX.X, ALU.add)\
                    .then_inc(summed, 1)

            def skip(c, half, g, s, k):
                dve.wait_ge(summed, unit_no(c, half, g, s, k) + 1)
                dve.scalar_tensor_tensor(out=yt[:, k], in0=unit[:, k, 1], scalar=par[:, bass.ds(chan(g, s, k) + C_D, 1)],
                                         in1=yt[:, k], op0=ALU.mult, op1=ALU.add).then_inc(skipped, 1)

            def gate(c, half, g, s, k):
                dve.wait_ge(skipped, unit_no(c, half, g, s, k) + 1)
                dve.tensor_tensor(yt[:, k], yt[:, k], unit[:, k, 2], ALU.mult).then_inc(unit_done, 1)

            def convolution(e, g, s, mring, *moffs):
                pair = g * S4 + (e * 8 + s)
                for j in range(K):
                    for k in range(2):
                        ch = chan(g, s, k)
                        w = par[:, bass.ds(ch * K + (C_CONVW + j), 1)]
                        if j == 0:
                            dve.wait_ge(evacuated[mring.slot(moffs[k])], mring.turn(g, moffs[k]) + 2)
                            dve.wait_ge(ut_stored[k], 16 * (ut_turn(e, 0, g, s) + 1))
                            dve.wait_ge(wssm_used, ch + (e * DT + 1))
                            ins = dve.tensor_scalar(ut[:, k], xin[:, k, 0:TC], w, None, ALU.mult)
                        else:
                            dve.wait_ge(conv_tap, pair * 6 + (2 * (j - 1) + k + 1))
                            ins = dve.scalar_tensor_tensor(out=ut[:, k], in0=xin[:, k, j:j + TC], scalar=w,
                                                           in1=ut[:, k], op0=ALU.mult, op1=ALU.add)
                        ins.then_inc(conv_tap if j < K - 1 else conv_done, 1)

            def output_add(c, half, g, s, k):
                wring, mring = w_ring(c, half), m_ring(c, half)
                b = mring.slot(m_off(c, s, "ffn", k))
                m = 4 * (s - 2) + k
                dve.wait_ge(product_done, wring.number(g, w_off(c, half, g, s, "ffn", k)) + W_DONE)
                dve.wait_ge(facc_zero, c + 1)
                dve.tensor_tensor(facc[:, m], pm[b][:, :], facc[:, m], ALU.add).then_inc(evacuated[b], 1)

            def combine(ring, off, e, g, s, base):
                idx = g * 2 + (HT * e + base + s // 2)
                dve.wait_ge(product_done, ring.number(g, off) + W_DONE)
                dve.wait_ge(gx_in, idx * 32 + 32)
                n = out_tokens(e)
                dve.tensor_tensor(gx[:, 0, 0:n], p_out[:, 0:n], gx[:, 0, 0:n], ALU.mult).then_inc(d_free, 1)
                dve.wait_ge(d_free, idx + 2)
                dve.tensor_tensor(gx[:, 0, 0:n], gx[:, 0, 0:n], gx[:, 1, 0:n], ALU.add).then_inc(out_ready, 1)

            def combine_rest(g, s):
                c, half, b = NCH - 1, 0, s % 2
                dve.wait_ge(product_done, w_ring(c, half).number(g, w_off(c, half, g, s, "rest", 1)) + W_DONE)
                dve.wait_ge(rest_in[b], g * 64 + (32 * (s // 2) + 32))
                dve.tensor_tensor(dtb[:, b, 0:TS], p_st[b][:, 0:TS], dtb[:, b, 0:TS], ALU.mult).then_inc(last_free, 1)
                dve.wait_ge(last_free, g * S4 + (s + DONE))
                dve.tensor_tensor(dtb[:, b, 0:TS], dtb[:, b, 0:TS], dtb[:, b, TS:], ALU.add).then_inc(rest_ready, 1)

            def pre_chained(g, s, i):
                dve.wait_ge(pre_chain, g * 24 + (6 * s + i))

            def pre_dt_arguments(g, s):
                z, r, _, _ = pre_dt(s)
                dve.wait_ge(pre_stored[s % 2], g * 64 + (32 * (s // 2) + 16))
                for k in range(2):
                    ch = chan(g, s, k)
                    dve.wait_ge(dt_full, ch + 1)
                    dve.tensor_scalar(z[:, k], p_st[k][:, :], par[:, bass.ds(ch + C_BDT, 1)], None, ALU.add)\
                        .then_inc(dt_bank_free, 1)
                dve.wait_ge(dt_bank_free, chan(g, s, 1) + DONE)
                dve.tensor_scalar(r, z, 0.0, None, ALU.max).then_inc(pre_chain, 1)
                pre_chained(g, s, 1)
                dve.scalar_tensor_tensor(out=z, in0=r, scalar=-2.0, in1=z, op0=ALU.mult, op1=ALU.add).then_inc(pre_chain, 1)

            def pre_dt_plus_one(g, s):
                _, _, p, w = pre_dt(s)
                dve.wait_ge(pre_exp, g * S4 + (s + 1))
                dve.tensor_scalar(w, p, 1.0, None, ALU.add).then_inc(pre_chain, 1)
                pre_chained(g, s, 3)
                dve.scalar_tensor_tensor(out=p, in0=w, scalar=-1.0, in1=p, op0=ALU.add, op1=ALU.subtract).then_inc(pre_chain, 1)

            def pre_dt_sums(g, s):
                z, r, p, _ = pre_dt(s)
                dve.wait_ge(pre_ln, g * S4 + (s + 1))
                pre_chained(g, s, 4)
                dve.tensor_tensor(z, z, p, ALU.subtract).then_inc(pre_chain, 1)
                pre_chained(g, s, 5)
                dve.tensor_tensor(z, z, r, ALU.add).then_inc(pre_chain, 1)

            def dt_tile(e, g, s, k):
                n = chan(g, s, k) + (e - 1) * DT
                dve.wait_ge(dt_chain, n * 3 + 3)
                dve.scalar_tensor_tensor(out=dtb[:, 1], in0=dtb[:, 2], scalar=-1.0, in1=dtb[:, 1], op0=ALU.add,
                                         op1=ALU.subtract).then_inc(dt_sum, 1)
                dve.wait_ge(dt_sum, n * 3 + 4)
                dve.tensor_tensor(dtb[:, 3], dtb[:, 3], dtb[:, 1], ALU.subtract).then_inc(dt_sum, 1)
                dve.wait_ge(dt_sum, n * 3 + 5)
                dve.wait_ge(dt_stored, n * 16 + 16)
                dve.tensor_tensor(dtb[:, 4], dtb[:, 3], dtb[:, 0], ALU.add).then_inc(dt_sum, 1)

            def center(e):
                dve.wait_ge(mean_full, e + 1)
                for k in range(HT):
                    dve.tensor_tensor(xn[e % 2][:, k], xn[e % 2][:, k], p_st[0][:, :], ALU.subtract).then_inc(centered, 1)

            def normalise(e):
                x = xn[e % 2][:, :, :]
                dve.wait_ge(std_full, e + 1)
                dve.reciprocal(dtb[:, 2], dtb[:, 2]).then_inc(rstd_full, 1)
                dve.wait_ge(rstd_full, e + 1)
                dve.tensor_tensor(x, x, dtb[:, 2].unsqueeze(1).to_broadcast([P, HT, TC]), ALU.mult)\
                    .then_inc(xn_ready, 1)

            def ssm_norm(e):
                dve.wait_ge(srs_full, e + 1)
                dve.reciprocal(dtb[0:SROWS, 3], dtb[0:SROWS, 3]).then_inc(srs_inv, 1)
                dve.wait_ge(srs_inv, e + 1)
                dve.tensor_tensor(ssm[:, :], ssm[:, :], dtb[0:SROWS, 3], ALU.mult).then_inc(ssm_ready, 1)

            dve.sem_inc(product_done, NW)
            dve.sem_inc(dt_sum, 3)
            for free in (*evacuated, d_free, late_full):
                dve.sem_inc(free, 1)
            for free in (conv_done, wssm_used, dt_bank_free, unit_done, last_free):
                dve.sem_inc(free, 2)
            dve.memset(zeros[:, :], 0.0).then_inc(zeros_set, 1)
            for k in range(2):
                dve.memset(decay[:, k, :, 0:1], 0.0).then_inc(decay_free, 1)
            dve.wait_ge(aneg_exp, 1)
            dve.tensor_scalar(aneg[:, :], aneg[:, :], -1.0, None, ALU.mult).then_inc(aneg_full, 1)
            center(0)
            normalise(0)
            center(1)
            ring = pre_ring(0)
            with dve.Fori(0, 2) as g:
                for s in range(S4):
                    convolution(0, g, s, ring, 2 * s, 2 * s + 1)
            ssm_norm(0)
            normalise(1)
            for s in range(S4):
                pre_dt_arguments(0, s)
                pre_dt_plus_one(0, s)
                pre_dt_sums(0, s)

            for c in range(NCH):
                more = c < NCH - 1
                for half in range(2):
                    def steps(g):
                        for s in range(S4):
                            scan_first(c, half, g, s, 0, (s - 1, 1) if s > 0 else None)
                            if more and half == 1 and s == 1:
                                dt_tile(c + 1, g, 0, 1)
                            scan_rest(c, half, g, s, 0)
                            if more and half == 1 and s > 0:
                                dt_tile(c + 1, g, s, 0)
                            before = late_before(c, half, g, s)
                            if before is not None:
                                pre_dt_arguments(1, before)
                            if s >= 2:
                                output_add(c, half, g, s, 0)
                            scan_first(c, half, g, s, 1, (s, 0))
                            if more and half == 0:
                                convolution(c + 1, g, s, m_ring(c, half), m_off(c, s, "in", 0), m_off(c, s, "in", 1))
                            if before is not None:
                                pre_dt_plus_one(1, before)
                            if s >= 2:
                                output_add(c, half, g, s, 1)
                            if not more and half == 0:
                                combine_rest(g, s)
                            scan_rest(c, half, g, s, 1)
                            if before is not None:
                                pre_dt_sums(1, before)
                            if s == S4 - 1:
                                skip(c, half, g, s, 1)
                                gate(c, half, g, s, 1)
                            if more and half == 1:
                                dt_tile(c + 1, g, s, 0 if s == 0 else 1)
                            if s >= 2:
                                output_add(c, half, g, s, 2)
                                output_add(c, half, g, s, 3)
                            if c > 0 and s % 2:
                                combine(w_ring(c, half), w_off(c, half, g, s, "out"), c - 1, g, s, 4 * half)
                    steps_of(dve, c, half, steps)
                    if more and half == 0:
                        ssm_norm(c + 1)
                if c + 2 < NCH:
                    center(c + 2)
                    normalise(c + 2)
            dve.wait_ge(g_full, NCH)
            dve.wait_ge(resid_in, 16)
            dve.wait_ge(last_free, 2 * HT + 2)
            dve.tensor_tensor(early, early, facc[:, :, 0:TS], ALU.mult).then_inc(early_full, 1)
            dve.wait_ge(early_full, 1)
            dve.tensor_tensor(early, early, resid[:, :, 0:TS], ALU.add).then_inc(early_ready, 1)
            for m in range(HT):
                dve.wait_ge(product_done, last_ring.number(0, HT + m) + W_DONE)
                dve.tensor_tensor(facc[:, m, TS:], p_last[m][:, 0:TS], facc[:, m, TS:], ALU.mult).then_inc(last_scaled, 1)
                dve.wait_ge(last_scaled, m + 1)
                dve.tensor_tensor(facc[:, m, TS:], facc[:, m, TS:], resid[:, m, TS:], ALU.add).then_inc(last_ready, 1)

        @block.gpsimd
        def _(pool):
            def store_input(e, half, g, s):
                for k in range(2):
                    ch = chan(g, s, k)
                    if half == 0:
                        wait(pool, u_full, ch + (e * DT + 1))
                    else:
                        wait(pool, gate_full, gate_count(e, g, s, k))
                    pool.dma_start(spill[ch, :, 1 + half, toks(e)], ut[:, k]).then_inc(ut_stored[k], 16)

            def store_dt(e, g, s, k):
                ch = chan(g, s, k)
                n = ch + (e - 1) * DT
                wait(pool, dt_sum, n * 3 + 6)
                pool.dma_start(spill[ch, :, 0, toks(e)], dtb[:, 4]).then_inc(dt_stored, 16)

            def store_pre_dt(g, s):
                pool.wait_ge(pre_chain, g * 24 + (6 * s + 6))
                for k in range(2):
                    pool.dma_start(spill[chan(g, s, k), :, 0, toks(0)], pre_dt(s)[0][:, k]).then_inc(pre_stored[s % 2], 16)

            def store_late_gate(s, k):
                pool.wait_ge(late_full, 2 * s + k + 2)
                pool.dma_start(spill[chan(1, s, k), :, 2, toks(0)], gx[:, k]).then_inc(late_stored[k], 16)

            def store_bc(e):
                wait(pool, ssm_ready, e + 1)
                pool.dma_start(bc_d[:, toks(e)], ssm[R:SROWS, :]).then_inc(bc_stored, 16)

            def store_y(c, half, g, s, k):
                t0 = c * TC + half * TS
                wait(pool, unit_done, unit_no(c, half, g, s, k) + DONE)
                pool.dma_start(y_d[chan(g, s, k), :, t0:t0 + TS], yt[:, k]).then_inc(y_stored[k], 16)

            def load_gx(e, g, s, base):
                m = g * 2 + (base + s // 2)
                wait(pool, out_stored, (m + (HT * e + 1)) * 16)
                n = out_tokens(e)
                pool.dma_start(gx[:, 0, 0:n], g_d[m, :, e * TC:e * TC + n]).then_inc(gx_in, 16)
                pool.dma_start(gx[:, 1, 0:n], xT[m, :, e * TC:e * TC + n]).then_inc(gx_in, 16)

            def store_out(e, g, s, base):
                m = g * 2 + (base + s // 2)
                wait(pool, out_ready, m + (HT * e + 1))
                n = out_tokens(e)
                pool.dma_start(outT[m, :, e * TC:e * TC + n], gx[:, 0, 0:n]).then_inc(out_stored, 16)

            def load_rest(g, s):
                m, b = g * S4 + s, s % 2
                wait(pool, rest_stored[b], g * 32 + (16 * (s // 2) + 16))
                pool.dma_start(dtb[:, b, 0:TS], g_d[m, :, t_rest:t_rest + TS]).then_inc(rest_in[b], 16)
                pool.dma_start(dtb[:, b, TS:], xT[m, :, t_rest:t_rest + TS]).then_inc(rest_in[b], 16)

            def store_rest(g, s):
                m, b = g * S4 + s, s % 2
                wait(pool, rest_ready, m + 1)
                pool.dma_start(outT[m, :, t_rest:t_rest + TS], dtb[:, b, 0:TS]).then_inc(rest_stored[b], 16)

            def load_y_rest():
                wait(pool, product_done, w_ring(NCH - 2, 1).number(1, w_off(NCH - 2, 1, 1, 1, "ffn", 3)) + W_DONE)
                pool.dma_start(y_rest, y_d[:, :, t_rest:t_rest + TS].rearrange("k p t -> p k t")).then_inc(y_rest_in, 16)

            def load_y(c):
                for k in range(2):
                    wait(pool, y_stored[k], 16 * (STEPS * (c + 1) + 1))
                if c > 0:
                    wait(pool, product_done, w_ring(c, 1).number(1, w_off(c, 1, 1, 3, "out")) + W_DONE)
                pool.dma_start(yin[:, :, :], y_d[:, :, toks(c)].rearrange("k p t -> p k t")).then_inc(y_in, 16)

            def load_y_early():
                c = NCH - 1
                for k in range(2):
                    wait(pool, y_stored[k], 16 * (STEPS * c + 8 + 1))
                wait(pool, product_done, w_ring(c, 0).number(1, w_off(c, 0, 1, 3, "rest", 1)) + W_DONE)
                pool.dma_start(y_early, y_d[:, :, T - TC:T - TS].rearrange("k p t -> p k t")).then_inc(y_early_in, 16)

            for buf, stored in ((ut[:, 0], ut_stored[0]), (ut[:, 1], ut_stored[1]), (dtb[:, 4], dt_stored),
                                (yin[:, 0], pre_stored[0]), (yin[:, 8], pre_stored[1]),
                                (yt[:, 0], y_stored[0]), (yt[:, 1], y_stored[1]), (gx[:, 0, 2:], out_stored),
                                (gx[:, 0], late_stored[0]), (gx[:, 1], late_stored[1])):
                pool.dma_start(buf[:, 0:2], params[:, 0:2]).then_inc(stored, 16)
            pool.memset(facc[:, :, :], 0.0).then_inc(facc_zero, 1)
            with pool.Fori(0, 2) as g:
                for s in range(S4):
                    store_input(0, 0, g, s)
            store_bc(0)
            for s in range(S4):
                store_input(0, 1, 0, s)
                store_pre_dt(0, s)

            for c in range(NCH):
                more = c < NCH - 1
                for half in range(2):
                    def steps(g):
                        for s in range(S4):
                            if c > 0 and s % 2 == 0:
                                load_gx(c - 1, g, s, 4 * half)
                            if not more and half == 0:
                                load_rest(g, s)
                            before = late_before(c, half, g, s)
                            if before is not None:
                                store_late_gate(before, 1)
                            if more and half == 1 and s == 1:
                                store_dt(c + 1, g, 0, 1)
                            if more and half == 1 and s > 0:
                                store_dt(c + 1, g, s, 0)
                            store_y(c, half, g, s, 0)
                            if more:
                                store_input(c + 1, half, g, s)
                            if late_in(c, half, g):
                                store_late_gate(s, 0)
                            if before is not None:
                                store_pre_dt(1, before)
                            if more and half == 1:
                                store_dt(c + 1, g, s, 0 if s == 0 else 1)
                            if not more and half == 0:
                                store_rest(g, s)
                            store_y(c, half, g, s, 1)
                            if c > 0 and s % 2:
                                store_out(c - 1, g, s, 4 * half)
                    steps_of(pool, c, half, steps)
                    if half == 0:
                        if more:
                            store_bc(c + 1)
                        else:
                            load_y_early()
                if c == NCH - 2:
                    load_y_rest()
                    for b in range(2):
                        wait(pool, dt_stored, 16 * (DT * (NCH - 1) + 1))
                        pool.dma_start(dtb[:, b, 0:2], params[:, 0:2]).then_inc(rest_stored[b], 16)
                if more:
                    load_y(c)
                    wait(pool, g_full, c + 1)
                    pool.dma_start(g_d[:, :, toks(c)].rearrange("m p t -> p m t"), facc[:, :, :]).then_inc(g_stored, 16)
                    wait(pool, g_stored, 16 * (c + 1))
                    pool.memset(facc[:, :, :], 0.0).then_inc(facc_zero, 1)
            wait(pool, out_stored, 16 * (HT * (NCH - 1) + 1))
            for stored in rest_stored:
                wait(pool, stored, 16 * (S4 + 1))


def kernel(**inputs):
    import numpy as np
    import concourse.bacc as bacc
    from concourse.bass_utils import run_bass_kernel_spmd

    def arr(name):
        return np.asarray(inputs[name])

    def tiles(w):
        k, m = w.shape
        w = w.reshape(k // H, 8, P, m // P, P).transpose(3, 0, 2, 1, 4)
        return np.ascontiguousarray(w).reshape(m // P, k // H, P, 8 * P)

    def channels(v, n):
        return v.reshape(-1, P, n).transpose(1, 0, 2).reshape(P, -1)

    x = arr("L0_attn_hidden_states")
    w_in = arr("L0_attn_W_in").T
    blk = np.zeros((P, SROWS), np.float32)
    for a, n in ((0, R), (R, N), (R + N, N)):
        blk[a:a + n, a:a + n] = 1.0 / n
    consts = np.zeros((P, NPAR - C_ONES), np.float32)
    consts[:, 0:P] = 1.0 / H
    consts[:, C_BLK - C_ONES:C_BLK - C_ONES + SROWS] = blk
    consts[:, C_EPS - C_ONES] = LN_EPS
    consts[:, C_EPS - C_ONES + 1] = RMS_EPS
    params = np.concatenate([
        channels(arr("L0_attn_conv_w"), K), channels(arr("L0_attn_conv_b"), 1), channels(arr("L0_attn_b_dt"), 1),
        channels(arr("L0_attn_D"), 1), channels(arr("L0_attn_A_log"), N), channels(arr("L0_ffn_inter_b"), 1),
        channels(arr("L0_ffn_output_b"), 1), consts], axis=1)
    arrays = {
        "xT": np.ascontiguousarray(x.reshape(T, H).T).reshape(HT, P, T),
        "params": np.ascontiguousarray(params),
        "w_x": tiles(w_in[:, :D_IN])[:, 0],
        "w_g": tiles(w_in[:, D_IN:])[:, 0],
        "w_1": tiles(arr("L0_ffn_inter_w"))[:, 0],
        "w_2": np.ascontiguousarray(tiles(arr("L0_ffn_output_w")).transpose(1, 0, 2, 3)).reshape(FT, P, 8 * P),
        "w_o": tiles(arr("L0_attn_W_out").T).reshape(DT, P, 8 * P),
        "w_ssm": np.ascontiguousarray(arr("L0_attn_W_x").T).reshape(DT, P, SROWS),
        "w_dt": np.ascontiguousarray(arr("L0_attn_W_dt").reshape(DT, P, R).transpose(0, 2, 1)),
    }
    nc = bacc.Bacc("TRN2", target_bir_lowering=False, num_devices=1)
    args = {}
    maps = {}
    for name, a in arrays.items():
        maps[f"in_{name}"] = np.ascontiguousarray(a)
        args[name] = nc.dram_tensor(f"in_{name}", a.shape, mybir.dt.from_np(a.dtype), kind="ExternalInput").ap()
    args["outT"] = nc.dram_tensor("out_0", (HT, P, T), F32, kind="ExternalOutput").ap()
    build(nc, **args)
    r = run_bass_kernel_spmd(nc, [maps], core_ids=[0])
    got = r.results[0]["out_0"]
    return np.ascontiguousarray(np.asarray(got).reshape(H, T).T).reshape(B, L, H)
```
